# Optimizing a Trainium2 kernel written in Bass

```python
import numpy as np
import jax
import jax.numpy as jnp

def _softmax(x, axis=-1):
    return jax.nn.softmax(x, axis=axis)

def _gelu(x):
    return jax.nn.gelu(x, approximate=True)

def _silu(x):
    return jax.nn.silu(x)

def _sigmoid(x):
    return jax.nn.sigmoid(x)

def _layernorm(x, axis=-1, eps=1e-05):
    m = jnp.mean(x, axis=axis, keepdims=True)
    v = jnp.var(x, axis=axis, keepdims=True)
    return (x - m) / jnp.sqrt(v + eps)

def _scatter_add(tgt, idx, src, axis=0):
    return tgt.at[idx].add(src)

def _segment_sum(src, seg, n):
    return jax.ops.segment_sum(src, seg, n)
kernel_name = 'mk_flamingo_gated_d1_seqx_r4_95759a'

def setup_inputs(seed: int=0):
    np.random.seed(seed)
    _w = jnp.asarray

    def _rec_inputs():
        import jax
        import jax.numpy as jnp
        _rk = jax.random.key(seed)
        x = 7.22e-05 + 1 * jax.random.normal(jax.random.fold_in(_rk, 1), (16, 128, 512), jnp.float32)
        _lenS = 128 - jax.random.randint(jax.random.fold_in(_rk, 7), (16,), 0, max(1, 128 // 4) + 1, jnp.int32)
        _lenS2 = 128 - jax.random.randint(jax.random.fold_in(_rk, 8), (16,), 0, max(1, 128 // 4) + 1, jnp.int32)
        _ctx_2048P = jax.random.normal(jax.random.fold_in(_rk, 11), (16, 16, 512), jnp.float32)
        _ctx_2048c = jax.random.dirichlet(jax.random.fold_in(_rk, 511), 0.3 * jnp.ones((16,), jnp.float32), (16, 128))
        _ctx_2048t = jnp.einsum('bsk,bkd->bsd', _ctx_2048c, _ctx_2048P)
        _ctx_2048t = _ctx_2048t * jax.lax.rsqrt(jnp.mean(jnp.square(_ctx_2048t)) + 1e-12) * 0.953939
        ctx_2048 = 4.13588e-05 + 0.999923 * (_ctx_2048t + 0.3 * jax.random.normal(jax.random.fold_in(_rk, 611), (16, 128, 512), jnp.float32))
        _g = jax.random.normal(jax.random.fold_in(_rk, 9001), (2, 1), jnp.float32)
        _g = jnp.sign(_g) * jnp.maximum(jnp.abs(_g), 1.0) + (_g == 0) * 1.0
        g_xattn = _g[0]
        g_ffn = _g[1]
        return (x, ctx_2048, g_xattn, g_ffn)
    x, ctx_2048, g_xattn, g_ffn = _rec_inputs()

    def _L0_xattn_setup():
        import jax, jax.numpy as jnp
        import numpy as np
        N_HEAD = 8
        key = jax.random.key(seed)
        k1, k2, k3 = jax.random.split(key, 3)
        b, d, m = (4, 256, 512)
        c, n = (256, 512)
        q = jax.random.normal(k1, (b, d, m), dtype=jnp.float32)
        k = jax.random.normal(k2, (d // d * b, d, n), dtype=jnp.float32).reshape(b, d, n)
        v = jax.random.normal(k3, (b, c, n), dtype=jnp.float32)
        return {'q': q, 'k': k, 'v': v}
    _L0_xattn_all = _L0_xattn_setup()
    _L0_xattn_in = {k: v for k, v in _L0_xattn_all.items() if k in ()}
    del _L0_xattn_all

    def _L0_ffn_setup():
        import jax, jax.numpy as jnp
        import numpy as np
        B, S, H, E = (4, 512, 512, 8)
        key = jax.random.key(seed)
        k_x, k_wg, k_w, k_b = jax.random.split(key, 4)
        x = jax.random.normal(k_x, (B, S, H), dtype=jnp.float32)
        wg = jax.random.normal(k_wg, (H, E), dtype=jnp.float32) * (1.0 / np.sqrt(H))
        W = jax.random.normal(k_w, (E, H, H), dtype=jnp.float32) * (1.0 / np.sqrt(H))
        b = jax.random.normal(k_b, (E, H), dtype=jnp.float32) * 0.01
        return {'x': x, 'wg': wg, 'W': W, 'b': b}
    _L0_ffn_all = _L0_ffn_setup()
    _L0_ffn_in = {k: v for k, v in _L0_ffn_all.items() if k in ('wg', 'W', 'b')}
    del _L0_ffn_all
    return {'x': x, 'ctx_2048': ctx_2048, 'g_xattn': g_xattn, 'g_ffn': g_ffn, 'L0_ffn_wg': _L0_ffn_in['wg'], 'L0_ffn_W': _L0_ffn_in['W'], 'L0_ffn_b': _L0_ffn_in['b']}

def reference(x, ctx_2048, g_xattn, g_ffn, L0_ffn_wg, L0_ffn_W, L0_ffn_b):
    import jax
    import jax.numpy as jnp

    def _L0_xattn_ref(q, k, v):
        import jax, jax.numpy as jnp
        import numpy as np
        N_HEAD = 8
        b, d, m = q.shape
        c = v.shape[1]
        h = N_HEAD
        qh = q.reshape(b * h, d // h, m)
        kh = k.reshape(b * h, d // h, -1)
        vh = v.reshape(b * h, c // h, -1)
        scale = 1.0 / jnp.sqrt(jnp.asarray(d // h, dtype=q.dtype))
        qk = jnp.einsum('bdm,bdn->bmn', qh, kh) * scale
        sm = jax.nn.softmax(qk, axis=-1)
        ret = jnp.einsum('bmn,bcn->bcm', sm, vh)
        return ret.reshape(b, c, m)

    def _L0_ffn_ref(x, wg, W, b):
        import jax, jax.numpy as jnp
        import numpy as np
        B, S, H, E = (4, 512, 512, 8)
        Bv, Sv, Hv = x.shape
        Ev = W.shape[0]
        xt = x.reshape(-1, Hv)
        logits = xt @ wg
        probs = jax.nn.softmax(logits, axis=-1)
        idx = jnp.argmax(probs, axis=-1)
        gate = jnp.take_along_axis(probs, idx[:, None], axis=1)
        onehot = jax.nn.one_hot(idx, Ev, dtype=x.dtype)
        expert_out = jnp.einsum('nh,eoh->neo', xt, W) + b[None, :, :]
        combine = onehot * gate
        out = jnp.einsum('ne,neo->no', combine, expert_out)
        return out.reshape(Bv, Sv, Hv)
    x = x + jnp.tanh(g_xattn[0]) * _L0_xattn_ref(_layernorm(x, axis=-1), ctx_2048, ctx_2048)
    x = x + jnp.tanh(g_ffn[0]) * _L0_ffn_ref(_layernorm(x, axis=-1), L0_ffn_wg, L0_ffn_W, L0_ffn_b)
    return x

_drawn_inputs = setup_inputs


def setup_inputs(seed=0):
    import zlib

    import numpy as np

    out = dict(_drawn_inputs(seed))
    spreads = {}
    factors = {'L0_ffn_b': 8.0}
    for name, (base, spread) in spreads.items():
        noise = np.random.default_rng([zlib.crc32(name.encode()), seed]).standard_normal(out[name].shape)
        drawn = base * np.exp(spread * noise) if base else spread * noise
        out[name] = jnp.asarray(drawn.astype(out[name].dtype))
    for name, factor in factors.items():
        out[name] = (out[name] * factor).astype(out[name].dtype)
    return out
```

```python
import concourse.bass as bass
from concourse import mybir
from contextlib import ExitStack

F32, BF16, I32, U32 = mybir.dt.float32, mybir.dt.bfloat16, mybir.dt.int32, mybir.dt.uint32
ALU = mybir.AluOpType
ACT = mybir.ActivationFunctionType
AX = mybir.AxisListType

NB, ROWS, DM = 16, 128, 512
NH, DH = 8, 16
NG, NJ = 2, 4
NC = DM // 128
STEPS = NG * NC
NP = 3
TERMS = 6
KS = TERMS * DH
KA = KS + NP
EPS = 1e-5
NE = 8
NT = NB * ROWS
CAP = NT
NSLOT = NT // 128 + NE - 1
NONE = 2 * NT
REC = 2 * DM + 4
NREC = 4
QTERM = [0, 0, 0, 1, 1, 2]
RING_FIRST, RING_BATCH = 34, 38
DVE_BATCH, POOL_BATCH = 15, 4


class Batch:

    def __init__(self, i, p):
        self.i, self.p = i + p // 2, p % 2
        self.b = self.i * 2 + self.p

    def plus(self, n):
        return Batch(self.i, self.p + n) if n >= 0 else Batch(self.i - 1, self.p + n + 2)


class Chain:

    def __init__(self, eng, sem):
        self.eng, self.sem, self.base, self.n = eng, sem, 0, 0

    def add(self, op):
        op.then_inc(self.sem, 1)
        self.n += 1

    def settle(self):
        self.eng.wait_ge(self.sem, self.base + self.n)


def wait(eng, sem, value):
    if not isinstance(value, int) or value > 0:
        eng.wait_ge(sem, value)


def stand_alone(eng):
    eng.nop(nofuse=True)


def ring_start(b):
    return RING_FIRST if isinstance(b, int) and b == 0 else b * RING_BATCH + (2 * RING_FIRST - RING_BATCH)


def build(nc, x_rows, x_perm, k_perm, v_t, w_t, wg_t, bias, g_attn, g_ffn, out):
    ctx = ExitStack()
    with ctx:
        def sb(name, shape, dt=F32):
            return ctx.enter_context(nc.sbuf_tensor(name, shape, dt))

        def sem(name):
            return ctx.enter_context(nc.semaphore(name))

        parts_dram = nc.dram_tensor("parts_dram", [NB, 2, NP, ROWS, DM], BF16, kind="Internal").ap()
        recs_dram = nc.dram_tensor("recs_dram", [NT, REC], F32, kind="Internal").ap()
        table_dram = nc.dram_tensor("table_dram", [NE * CAP, 1], I32, kind="Internal").ap()
        table_blocks = table_dram.rearrange("(k p) o -> k (p o)", p=128)

        identity = sb("identity", [128, 128])
        before = sb("before", [128, 128], BF16)
        ones_bf = sb("ones_bf", [128, 128], BF16)
        low_half = sb("low_half", [128, 1])
        high_half = sb("high_half", [128, 1])
        gates = sb("gates", [128, 4])
        low_gate = sb("low_gate", [128, 1])
        high_gate = sb("high_gate", [128, 1])
        power = sb("power", [128, 1])
        expert_iota = sb("expert_iota", [128, NE])
        block_iota = sb("block_iota", [128, NE, NB])
        up_to = sb("up_to", [128, NE, NE])
        slot_iota = sb("slot_iota", [128, 1])
        none_i = sb("none_i", [128, 128], I32)
        wg_sb = sb("wg_sb", [128, NC, NE])
        w_sb = sb("w_sb", [128, NC, NE, DM])
        xp_in = sb("xp_in", [128, DM])
        k_in = sb("k_in", [128, DM])
        v_in = sb("v_in", [128, NC, NG, NJ, DH])
        x_in = sb("x_in", [128, DM])
        qn = sb("qn", [128, DM])
        resid = sb("resid", [128, 2, DM])
        parts = sb("parts", [128, 2, NP, DM], BF16)
        q_stack = sb("q_stack", [128, 2, NG, NJ, DM], BF16)
        k_stack = sb("k_stack", [128, 2, NG, NJ, DM], BF16)
        v_ones = sb("v_ones", [128, 2, NC, NG, NJ, 2 * DH])
        neg_max = sb("neg_max", [128, NG, NJ, NC])
        shift_rest = sb("shift_rest", [NJ * NC, NG, 128])
        shift_parts = sb("shift_parts", [NJ * NC, NG, NP, 128], BF16)
        probs = sb("probs", [128, 2, NJ, DM])
        low_num = sb("low_num", [128, DM])
        low_den = sb("low_den", [128, DM])
        num = sb("num", [128, DM])
        den = sb("den", [128, DM])
        den_own = sb("den_own", [128, DM])
        rec = sb("rec", [128, REC])
        xt = sb("xt", [128, 2, NC, 128])
        st1 = sb("st1", [128, 6])
        mv1 = sb("mv1", [128, 2])
        rs1 = sb("rs1", [128, 2])
        st2 = sb("st2", [128, 6])
        mv2 = sb("mv2", [128, 2])
        rs2 = sb("rs2", [128, 2])
        logits = sb("logits", [128, NE])
        top = sb("top", [128, 8])
        top_at = sb("top_at", [128, 8], U32)
        top_f = sb("top_f", [128, 1])
        neg_top = sb("neg_top", [128, 1])
        gate_exp = sb("gate_exp", [128, NE])
        gate_sum = sb("gate_sum", [128, 1])
        gate_inv = sb("gate_inv", [128, 1])
        onehot = sb("onehot", [128, NE], BF16)
        place = sb("place", [128, NE])
        dest_f = sb("dest_f", [128, 1])
        dest_i = sb("dest_i", [128, 1], I32)
        token_f = sb("token_f", [128, 1])
        token_i = sb("token_i", [128, 1], I32)
        count = sb("count", [128, NE])
        ffn_rec = k_stack[:].rearrange("p a g j m -> p (a g j m)").bitcast(F32)
        q_flat = q_stack[:].rearrange("p a g j m -> p (a g j m)").bitcast(F32)
        bias_sb = q_flat[:, 0:NE * DM].rearrange("p (e n) -> p e n", e=NE)
        rec_buf = sb("rec_buf", [128, REC])
        recs_in = [probs[:].rearrange("p a j m -> p (a j m)")[:, r * REC:(r + 1) * REC] for r in range(3)]
        recs_in.append(rec_buf[:])
        y_sum = [v_ones[:].rearrange("p a c g j d -> p (a c g j d)")[:, r * DM:(r + 1) * DM] for r in range(2)]
        y_out = [ffn_rec[:, r * DM:(r + 1) * DM] for r in range(NREC)]
        counts_n = sb("counts_n", [128, NE])
        fill = sb("fill", [128, NE, NB])
        tiles = sb("tiles", [128, NE])
        tri = sb("tri", [128, NE, NE])
        ends = sb("ends", [128, NE])
        passed = sb("passed", [128, NE])
        slot_f = sb("slot_f", [128, 4])
        slot_block = sb("slot_block", [128, 1], I32)
        slot_expert = sb("slot_expert", [1, 128], I32)
        slot_tokens = sb("slot_tokens", [32, 128], I32)
        slot_tokens_f = sb("slot_tokens_f", [32, 128])
        token_cols = sb("token_cols", [128, 32], I32)

        ps_scores = ctx.enter_context(nc.psum_tensor("ps_scores", [128, 2, 2, DM], F32))
        ps_ring = ctx.enter_context(nc.psum_tensor("ps_ring", [128, 2, DM], F32))
        ps_pv = ctx.enter_context(nc.psum_tensor("ps_pv", [128, NG, DM], F32))
        ps_y = ps_scores[:, 0]
        ps_xt = ps_scores[:, 1]

        consts_in = sem("consts_in")
        table_set = sem("table_set")
        xk_in = sem("xk_in")
        v_loaded = sem("v_loaded")
        x_loaded = sem("x_loaded")
        w_loaded = sem("w_loaded")
        parts_out = sem("parts_out")
        stack_in = [[sem(f"stack_in{p}{g}") for g in range(NG)] for p in range(2)]
        shift_in = [sem(f"shift_in{g}") for g in range(NG)]
        rec_out = sem("rec_out")
        table_out = sem("table_out")
        pool_const = sem("pool_const")
        dve_const = sem("dve_const")
        gates_ready = sem("gates_ready")
        ln1_stats, ln1_rstd, qn_ready = sem("ln1_stats"), sem("ln1_rstd"), sem("qn_ready")
        high_cast, mid_cast = sem("high_cast"), sem("mid_cast")
        rest_ready, low_ready = sem("rest_ready"), sem("low_ready")
        v_ready = sem("v_ready")
        ring_full, ring_free = sem("ring_full"), sem("ring_free")
        shift_ready = sem("shift_ready")
        scores_ready, exp_done, pv_done = sem("scores_ready"), sem("exp_done"), sem("pv_done")
        low_read, high_read = sem("low_read"), sem("high_read")
        recip_ready, x1_done = sem("recip_ready"), sem("x1_done")
        ln2_stats, ln2_rstd, xn2_ready = sem("ln2_stats"), sem("ln2_rstd"), sem("xn2_ready")
        top_ready, gate_summed = sem("top_ready"), sem("gate_summed")
        onehot_ready, dest_ready, gate_ready = sem("onehot_ready"), sem("dest_ready"), sem("gate_ready")
        dve_chain, pool_chain = sem("dve_chain"), sem("pool_chain")
        bias_in = sem("bias_in")
        slots_ready, expert_ready = sem("slots_ready"), sem("expert_ready")
        tokens_in, tokens_f, cols_ready = sem("tokens_in"), sem("tokens_f"), sem("cols_ready")
        rec_in = [sem(f"rec_in{r}") for r in range(NREC)]
        f_xt_full, f_xt_ready = sem("f_xt_full"), sem("f_xt_ready")
        y_full, y_read, y_ready = sem("y_full"), sem("y_read"), sem("y_ready")
        y_stored = [sem(f"y_stored{r}") for r in range(NREC)]

        DVE_CONSTS = 15
        POOL_CONSTS = 12
        block = ctx.enter_context(nc.Block())

        def rounds(eng, emit, after_first=None):
            for n in range(2):
                emit(Batch(n // 2, n % 2), n > 0, True, True)
            start = after_first() if after_first else None
            with eng.Fori(1, 6) as i:
                for p in range(2):
                    B = Batch(i, p)
                    if start is not None:
                        start[0].base, start[0].n = (i - 1) * (2 * start[2]) + (start[1] + p * start[2]), 0
                    emit(B, True, True, True)
                    if start is not None:
                        assert start[0].n == start[2], (start[0].n, start[2])
            if start is not None:
                start[0].base, start[0].n = start[1] + 10 * start[2], 0
            for n in range(12, NB):
                emit(Batch(n // 2, n % 2), True, n + 1 < NB, n + 3 < NB)

        @block.sync
        def _(sp):
            def load_rows_keys(B):
                wait(sp, rest_ready, B.b * 2)
                if not isinstance(B.b, int):
                    stand_alone(sp)
                sp.dma_start(xp_in[:], x_perm[bass.ds(B.b, 1)].rearrange("o p m -> (o p) m")).then_inc(xk_in, 16)
                sp.dma_start(k_in[:], k_perm[bass.ds(B.b, 1)].rearrange("o p m -> (o p) m")).then_inc(xk_in, 16)

            def load_values(B):
                wait(sp, v_ready, B.b)
                if not isinstance(B.b, int):
                    stand_alone(sp)
                sp.dma_start(v_in[:].rearrange("p c g j d -> p (c g j d)"),
                             v_t[bass.ds(B.b, 1)].rearrange("o p m -> (o p) m")).then_inc(v_loaded, 16)

            def load_residual(B):
                wait(sp, x1_done, B.b)
                if not isinstance(B.b, int):
                    stand_alone(sp)
                sp.dma_start(x_in[:], x_rows[bass.ds(B.b, 1)].rearrange("o p m -> (o p) m")).then_inc(x_loaded, 16)

            def load_stack(B, g):
                wait(sp, parts_out, B.b * 16 + 16)
                if not isinstance(B.b, int):
                    stand_alone(sp)
                wait(sp, scores_ready, B.b * (2 * STEPS) + (STEPS * (g + 1) - 4 * STEPS))
                if not isinstance(B.b, int):
                    stand_alone(sp)
                mine = parts_dram[bass.ds(B.b, 1)].rearrange("o s t (c g j) m -> s (o g) t c (j m)", g=NG, j=NJ)
                for n, t in enumerate(QTERM):
                    sp.dma_start(q_stack[n * DH:(n + 1) * DH, B.p, g].rearrange("p j m -> p (j m)"),
                                 mine[0, g, t]).then_inc(stack_in[B.p][g], 16)
                for first, n in ((0, 3), (3, 2), (5, 1)):
                    sp.dma_start(k_stack[first * DH:(first + n) * DH, B.p, g].rearrange("p j m -> p (j m)"),
                                 mine[1, g, 0:n].rearrange("t c m -> (t c) m")).then_inc(stack_in[B.p][g], 16)

            def load_shift(B, g):
                sp.wait_ge(shift_ready, B.b * 2 + (g + 1))
                for t in range(NP):
                    sp.dma_start(q_stack[KS + t:KS + t + 1, B.p, g].rearrange("o j (c m) -> o (j c) m", c=NC),
                                 shift_parts[:, g, t]).then_inc(shift_in[g], 16)

            def load_weights(B):
                n = NC * NE * DM // NB
                sp.dma_start(w_sb[:].rearrange("p c e n -> p (c e n)")[:, bass.ds(B.b * n, n)],
                             w_t[bass.ds(B.b, 1)].rearrange("o p n -> (o p) n")).then_inc(w_loaded, 16)

            def store_record(B):
                sp.wait_ge(gate_ready, B.b + 1)
                stand_alone(sp)
                sp.dma_start(recs_dram[bass.ds(B.b * ROWS, ROWS)], rec[:]).then_inc(rec_out, 16)

            load_rows_keys(Batch(0, 0))
            sp.dma_start(gates[:, 0:1], g_attn.partition_broadcast(128)).then_inc(consts_in, 16)
            sp.dma_start(gates[:, 1:2], g_ffn.partition_broadcast(128)).then_inc(consts_in, 16)
            sp.dma_start(wg_sb[:].rearrange("p c e -> p (c e)"), wg_t).then_inc(consts_in, 16)
            load_values(Batch(0, 0))
            load_rows_keys(Batch(0, 1))
            for g in range(NG):
                load_stack(Batch(0, 0), g)
            load_rows_keys(Batch(1, 0))
            for g in range(NG):
                load_stack(Batch(0, 1), g)
            for g in range(NG):
                load_shift(Batch(0, 0), g)
            sp.wait_ge(pool_const, POOL_CONSTS)
            sp.dma_start(table_dram.rearrange("(k p) o -> k (p o)", p=128), none_i[:]).then_inc(table_set, 16)
            load_values(Batch(0, 1))

            def emit(B, prev, nxt, prep):
                if prep:
                    load_rows_keys(B.plus(3))
                load_weights(B)
                stack = not isinstance(B.b, int) or B.b + 2 < NB
                if stack:
                    load_stack(B.plus(2), 0)
                    load_values(B.plus(2))
                load_residual(B)
                if nxt:
                    load_shift(B.plus(1), 0)
                if stack:
                    load_stack(B.plus(2), 1)
                if nxt:
                    load_shift(B.plus(1), 1)
                if prev:
                    store_record(B.plus(-1))

            rounds(sp, emit)
            sp.wait_ge(scores_ready, 2 * STEPS * NB)
            sp.dma_start(bias_sb.rearrange("p e n -> p (e n)"), bias.partition_broadcast(128)).then_inc(bias_in, 16)
            store_record(Batch(7, 1))

        @block.gpsimd
        def _(pool):
            chain = Chain(pool, pool_chain)
            steps = [lambda: nc.gpsimd.memset(identity[:], 0.0),
                     lambda: nc.gpsimd.affine_select(out=identity[:], in_=identity[:], compare_op=ALU.not_equal, fill=1.0,
                                                     base=0, pattern=[[-1, 128]], channel_multiplier=1),
                     lambda: nc.gpsimd.memset(before[:], 1.0),
                     lambda: nc.gpsimd.affine_select(out=before[:], in_=before[:], compare_op=ALU.is_gt, fill=0.0,
                                                     base=0, pattern=[[1, 128]], channel_multiplier=-1),
                     lambda: nc.gpsimd.memset(ones_bf[:], 1.0),
                     lambda: nc.gpsimd.memset(power[:], -0.5),
                     lambda: nc.gpsimd.iota(none_i[:], [[0, 128]], base=NONE, channel_multiplier=0),
                     lambda: nc.gpsimd.iota(expert_iota[:], [[1, NE]], base=0, channel_multiplier=0,
                                            allow_small_or_imprecise_dtypes=True),
                     lambda: nc.gpsimd.iota(block_iota[:], [[0, NE], [128, NB]], base=0, channel_multiplier=0,
                                            allow_small_or_imprecise_dtypes=True),
                     lambda: nc.gpsimd.iota(slot_iota[:], [[0, 1]], base=0, channel_multiplier=1,
                                            allow_small_or_imprecise_dtypes=True),
                     lambda: nc.gpsimd.iota(token_f[:], [[0, 1]], base=0, channel_multiplier=1,
                                            allow_small_or_imprecise_dtypes=True),
                     lambda: nc.gpsimd.iota(count[:], [[CAP, NE]], base=0, channel_multiplier=0,
                                            allow_small_or_imprecise_dtypes=True)]
            assert len(steps) == POOL_CONSTS
            for n, step in enumerate(steps):
                step().then_inc(pool_const, 1)
                pool.wait_ge(pool_const, n + 1)

            def rstd(B, stats, mv, rs, done, scale):
                pool.wait_ge(stats, B.b + 1)
                stand_alone(pool)
                chain.add(nc.gpsimd.tensor_scalar(rs[:, 0:1], mv[:, 1:2], EPS, scale, ALU.add, ALU.mult))
                chain.settle()
                nc.gpsimd.tensor_tensor(rs[:, 1:2], rs[:, 0:1], power[:], ALU.pow).then_inc(done, 1)

            def rstd1(B):
                wait(pool, qn_ready, B.b)
                rstd(B, ln1_stats, mv1, rs1, ln1_rstd, float(DH))

            def rstd2(B):
                wait(pool, xn2_ready, B.b)
                rstd(B, ln2_stats, mv2, rs2, ln2_rstd, 1.0)

            def copy_values(B):
                pool.wait_ge(v_loaded, B.b * 16 + 16)
                wait(pool, pv_done, (B.b - 1) * STEPS)
                stand_alone(pool)
                chain.add(nc.gpsimd.tensor_copy(v_ones[:, B.p, :, 0, :, 0:DH], v_in[:, :, 0]))
                nc.gpsimd.tensor_copy(v_ones[:, B.p, :, 1, :, DH:2 * DH], v_in[:, :, 1]).then_inc(v_ready, 1)

            def rests(B):
                for s, src in enumerate((qn, k_in)):
                    pool.wait_ge(high_cast, B.b * 2 + (s + 1))
                    wait(pool, low_ready, B.b * 2)
                    nc.gpsimd.tensor_tensor(resid[:, s], src[:], parts[:, s, 0], ALU.subtract).then_inc(rest_ready, 1)

            def lows(B):
                for s in range(2):
                    pool.wait_ge(mid_cast, B.b * 2 + (s + 1))
                    nc.gpsimd.tensor_tensor(parts[:, s, 2], resid[:, s], parts[:, s, 1], ALU.subtract).then_inc(low_ready, 1)
                pool.wait_ge(low_ready, B.b * 2 + 2)
                pool.dma_start(parts_dram[bass.ds(B.b, 1)].rearrange("o s t p m -> p (o s t) m"),
                               parts[:].rearrange("p s t m -> p (s t) m")).then_inc(parts_out, 16)

            def add_attention(B):
                pool.wait_ge(recip_ready, B.b + 1)
                pool.wait_ge(x_loaded, B.b * 16 + 16)
                wait(pool, rec_out, B.b * 16)
                chain.add(nc.gpsimd.tensor_tensor(num[:], num[:], den[:], ALU.mult))
                chain.settle()
                nc.gpsimd.tensor_tensor(rec[:, DM:2 * DM], num[:], x_in[:], ALU.add).then_inc(x1_done, 1)

            def store_tokens(B):
                pool.wait_ge(dest_ready, B.b + 1)
                stand_alone(pool)
                if isinstance(B.b, int) and B.b == 0:
                    pool.wait_ge(table_set, 16)
                pool.indirect_dma_start(table_dram, bass.IndirectOffsetOnAxis(ap=dest_i[:, 0:1], axis=0),
                                        token_i[:], None).then_inc(table_out, 16)

            for n in range(3):
                B = Batch(n // 2, n % 2)
                rstd1(B)
                rests(B)
                lows(B)
                if n == 0:
                    pool.wait_ge(dve_const, DVE_CONSTS)
                    copy_values(B)

            def emit(B, prev, nxt, prep):
                if nxt:
                    copy_values(B.plus(1))
                if prep:
                    rstd1(B.plus(3))
                if prev:
                    add_attention(B.plus(-1))
                    rstd2(B.plus(-1))
                if prep:
                    rests(B.plus(3))
                    lows(B.plus(3))
                if prev:
                    store_tokens(B.plus(-1))

            rounds(pool, emit, lambda: (chain, chain.n, POOL_BATCH))
            last = Batch(7, 1)
            add_attention(last)
            rstd2(last)
            store_tokens(last)

            pool.wait_ge(slots_ready, 1)
            pool.wait_ge(table_out, 16 * NB)
            pool.indirect_dma_start(slot_tokens[:], None, table_blocks,
                                    bass.IndirectOffsetOnAxis(ap=slot_block[0:32, 0:1], axis=0),
                                    bounds_check=NE * CAP // 128 - 1, oob_is_err=False).then_inc(tokens_in, 16)
            pool.wait_ge(rec_out, 16 * NB)

            pool.wait_ge(cols_ready, 1)

            def gather(s, r):
                pool.indirect_dma_start(recs_in[r], None, recs_dram,
                                        bass.IndirectOffsetOnAxis(ap=token_cols[:, s:s + 1], axis=0),
                                        bounds_check=NT - 1, oob_is_err=False).then_inc(rec_in[r], 16)

            def scatter(s, r):
                pool.wait_ge(y_ready, s + 1)
                pool.indirect_dma_start(out, bass.IndirectOffsetOnAxis(ap=token_cols[:, s:s + 1], axis=0),
                                        y_out[r], None,
                                        bounds_check=NT - 1, oob_is_err=False).then_inc(y_stored[r], 16)

            for r in range(NREC):
                gather(r, r)
            for s in range(NSLOT):
                scatter(s, s % NREC)
                if s + NREC < NSLOT:
                    gather(s + NREC, s % NREC)
            for r in range(NREC):
                pool.wait_ge(y_stored[r], 16 * len(range(r, NSLOT, NREC)))

        @block.scalar
        def _(act):
            act.wait_ge(consts_in, 16 * 3)
            nc.scalar.activation(gates[:, 2:4], gates[:, 0:2], ACT.Tanh).then_inc(gates_ready, 1)

            def cast_high(B):
                for s, (src, ready, value) in enumerate(((qn, qn_ready, B.b + 1), (k_in, xk_in, B.b * 32 + 32))):
                    act.wait_ge(ready, value)
                    wait(act, parts_out, B.b * 16)
                    nc.scalar.copy(parts[:, s, 0], src[:]).then_inc(high_cast, 1)

            def cast_mid(B):
                for s in range(2):
                    act.wait_ge(rest_ready, B.b * 2 + (s + 1))
                    nc.scalar.copy(parts[:, s, 1], resid[:, s]).then_inc(mid_cast, 1)

            def read_low(B):
                act.wait_ge(pv_done, B.b * STEPS + NC)
                wait(act, high_read, B.b * 2)
                nc.scalar.mul(low_num[:], ps_pv[:, 0], low_gate[:]).then_inc(low_read, 1)
                nc.scalar.mul(low_den[:], ps_pv[:, 0], high_half[:]).then_inc(low_read, 1)

            def sum_gate(B):
                act.wait_ge(top_ready, B.b + 1)
                nc.scalar.activation(gate_exp[:], logits[:], ACT.Exp, bias=neg_top[:],
                                     accum_out=gate_sum[:]).then_inc(gate_summed, 1)

            def exps(B, k):
                for jp in range(2):
                    act.wait_ge(scores_ready, B.b * (2 * STEPS) + (2 * k + jp + 1))
                    if jp == 0:
                        wait(act, pv_done, B.b * STEPS + (k - 1))
                    nc.scalar.activation(probs[:, k % 2, 2 * jp:2 * jp + 2], ps_scores[:, jp], ACT.Exp).then_inc(exp_done, 1)

            for n in range(3):
                cast_high(Batch(n // 2, n % 2))
                cast_mid(Batch(n // 2, n % 2))
                if n == 0:
                    act.wait_ge(dve_const, DVE_CONSTS)

            def emit(B, prev, nxt, prep):
                for k in range(STEPS):
                    exps(B, k)
                    if k == 3 and prep:
                        cast_high(B.plus(3))
                    if k == 5:
                        read_low(B)
                    if k == 6 and prep:
                        cast_mid(B.plus(3))
                    if k == 7 and prev:
                        sum_gate(B.plus(-1))

            rounds(act, emit)
            sum_gate(Batch(7, 1))

            def evacuate(s, r):
                act.wait_ge(f_xt_full, s + 1)
                wait(act, y_full, s - 1)
                nc.scalar.copy(xt[:, r % 2].rearrange("p c n -> p (c n)"), ps_xt[:, r % 2]).then_inc(f_xt_ready, 1)

            evacuate(0, 0)
            with act.Fori(0, (NSLOT - 1) // 2) as i:
                for r in range(2):
                    evacuate(i * 2 + (r + 1), r + 1)

        @block.vector
        def _(dve):
            chain = Chain(dve, dve_chain)
            steps = [lambda: nc.vector.memset(v_ones[:].rearrange("p a c g j d -> p (a c g j d)"), 1.0),
                     lambda: nc.vector.memset(k_stack[96:96 + NP].rearrange("p a g j m -> p (a g j m)"), 1.0),
                     lambda: nc.vector.memset(low_half[:], 0.0)]
            steps += [lambda j=j: nc.vector.memset(low_half[32 * j:32 * j + DH], 1.0) for j in range(NJ)]
            steps += [lambda: nc.vector.tensor_scalar(high_half[:], low_half[:], -1.0, 1.0, ALU.mult, ALU.add),
                      lambda: nc.vector.memset(rec[:, 2 * DM:REC], 0.0),
                      lambda: nc.vector.memset(rec_buf[:], 0.0),
                      lambda: nc.vector.memset(slot_tokens_f[:], float(NONE)),
                      lambda: nc.vector.tensor_copy(slot_tokens[:], slot_tokens_f[:]),
                      lambda: nc.vector.tensor_scalar(low_gate[:], low_half[:], gates[:, 2:3], None, ALU.mult),
                      lambda: nc.vector.tensor_scalar(high_gate[:], high_half[:], gates[:, 2:3], None, ALU.mult),
                      lambda: nc.vector.memset(up_to[:], 0.0)]
            assert len(steps) == DVE_CONSTS
            for n, step in enumerate(steps):
                if n == 12:
                    dve.wait_ge(gates_ready, 1)
                step().then_inc(dve_const, 1)
                dve.wait_ge(dve_const, n + 1)
            for e in range(NE):
                chain.add(nc.vector.memset(up_to[:, e, 0:e + 1], 1.0))
            chain.settle()
            dve.wait_ge(pool_const, POOL_CONSTS)

            def stats1(B):
                dve.wait_ge(xk_in, B.b * 32 + 32)
                chain.add(nc.vector.bn_stats(st1[:], xp_in[:]))
                chain.settle()
                stand_alone(dve)
                nc.vector.bn_aggr(mv1[:], st1[:]).then_inc(ln1_stats, 1)

            def norm1(B):
                dve.wait_ge(ln1_stats, B.b + 1)
                dve.wait_ge(ln1_rstd, B.b + 1)
                wait(dve, high_cast, B.b * 2)
                wait(dve, rest_ready, B.b * 2)
                nc.vector.tensor_scalar(qn[:], xp_in[:], mv1[:, 0:1], rs1[:, 1:2], ALU.subtract, ALU.mult).then_inc(qn_ready, 1)

            def maxima(B, u, n, k):
                g, j = divmod(k, NJ)
                for c in range(NC):
                    dve.wait_ge(ring_full, u + (n + c + 1))
                    nc.vector.tensor_reduce(neg_max[:, g, j, c:c + 1], ps_ring[:, (n + c) % 2], AX.X, ALU.max,
                                            negate=True).then_inc(ring_free, 1)

            def split_maxima(B, u, n, g):
                src = ps_ring[0:NJ * NC, n % 2, 0:128]
                dve.wait_ge(ring_full, u + (n + 1))
                wait(dve, shift_in[g], B.b * 48)
                chain.add(nc.vector.tensor_copy(shift_parts[:, g, 0], src))
                chain.settle()
                nc.vector.tensor_tensor(shift_rest[:, g], src, shift_parts[:, g, 0], ALU.subtract).then_inc(ring_free, 1)
                dve.wait_ge(ring_free, u + (n + 1))
                chain.add(nc.vector.tensor_copy(shift_parts[:, g, 1], shift_rest[:, g]))
                chain.settle()
                nc.vector.tensor_tensor(shift_parts[:, g, 2], shift_rest[:, g], shift_parts[:, g, 1],
                                        ALU.subtract).then_inc(shift_ready, 1)

            def divide(B):
                dve.wait_ge(low_read, B.b * 2 + 2)
                dve.wait_ge(pv_done, B.b * STEPS + STEPS)
                wait(dve, x1_done, B.b)
                nc.vector.scalar_tensor_tensor(num[:], ps_pv[:, 1], high_gate[:], low_num[:], ALU.mult,
                                               ALU.add).then_inc(high_read, 1)
                nc.vector.scalar_tensor_tensor(den_own[:], ps_pv[:, 1], low_half[:], low_den[:], ALU.mult,
                                               ALU.add).then_inc(high_read, 1)
                dve.wait_ge(high_read, B.b * 2 + 2)
                stand_alone(dve)
                chain.add(nc.vector.stream_shuffle(den[:], den_own[:], [(p + DH) % 32 for p in range(32)]))
                chain.settle()
                nc.vector.reciprocal(den[:], den[:]).then_inc(recip_ready, 1)

            def stats2(B):
                dve.wait_ge(x1_done, B.b + 1)
                chain.add(nc.vector.bn_stats(st2[:], rec[:, DM:2 * DM]))
                chain.settle()
                stand_alone(dve)
                nc.vector.bn_aggr(mv2[:], st2[:]).then_inc(ln2_stats, 1)

            def norm2(B):
                dve.wait_ge(ln2_stats, B.b + 1)
                dve.wait_ge(ln2_rstd, B.b + 1)
                nc.vector.tensor_scalar(rec[:, 0:DM], rec[:, DM:2 * DM], mv2[:, 0:1], rs2[:, 1:2], ALU.subtract,
                                        ALU.mult).then_inc(xn2_ready, 1)

            def take_xt(B, u, n):
                dve.wait_ge(ring_full, u + (n + 1))
                nc.vector.tensor_copy(xt[:, 0].rearrange("p c n -> p (c n)"), ps_ring[:, n % 2]).then_inc(ring_free, 1)

            def choose(B, u, n):
                dve.wait_ge(ring_full, u + (n + 1))
                nc.vector.tensor_copy(logits[:], ps_ring[:, n % 2, 0:NE]).then_inc(ring_free, 1)
                dve.wait_ge(ring_free, u + (n + 1))
                stand_alone(dve)
                chain.add(nc.vector.max(top[:], logits[:]))
                chain.settle()
                nc.vector.tensor_scalar(neg_top[:], top[:, 0:1], -1.0, None, ALU.mult).then_inc(top_ready, 1)
                chain.add(nc.vector.max_index(top_at[:], top[:], logits[:]))
                chain.settle()
                chain.add(nc.vector.tensor_copy(top_f[:], top_at[:, 0:1]))
                chain.settle()
                nc.vector.tensor_scalar(onehot[:], expert_iota[:], top_f[:], None, ALU.is_equal).then_inc(onehot_ready, 1)

            def rank(B, u, n):
                dve.wait_ge(ring_full, u + (n + 1))
                dve.wait_ge(onehot_ready, B.b + 1)
                nc.vector.tensor_tensor(place[:], ps_ring[:, n % 2, 0:NE], count[:], ALU.add).then_inc(ring_free, 1)
                dve.wait_ge(ring_free, u + (n + 1))
                chain.add(nc.vector.tensor_tensor(place[:], place[:], onehot[:], ALU.mult))
                chain.settle()
                chain.add(nc.vector.reduce_sum(dest_f[:], place[:], AX.X))
                chain.settle()
                wait(dve, table_out, B.b * 16)
                chain.add(nc.vector.tensor_copy(dest_i[:], dest_f[:]))
                chain.add(nc.vector.tensor_copy(token_i[:], token_f[:]))
                chain.settle()
                nc.vector.tensor_scalar(token_f[:], token_f[:], float(ROWS), None, ALU.add).then_inc(dest_ready, 1)
                dve.wait_ge(ring_full, u + (n + 2))
                nc.vector.tensor_tensor(count[:], count[:], ps_ring[:, (n + 1) % 2, 0:NE], ALU.add).then_inc(ring_free, 1)
                dve.wait_ge(gate_summed, B.b + 1)
                chain.add(nc.vector.reciprocal(gate_inv[:], gate_sum[:]))
                chain.settle()
                nc.vector.tensor_scalar(rec[:, 2 * DM:2 * DM + 1], gate_inv[:], gates[:, 3:4], None,
                                        ALU.mult).then_inc(gate_ready, 1)

            def prepare(B):
                stats1(B)
                norm1(B)

            prepare(Batch(0, 0))
            prepare(Batch(0, 1))
            n = 0
            for k in range(STEPS):
                maxima(Batch(0, 0), 0, n, k)
                n += NC
                if k % NC == NC - 1:
                    split_maxima(Batch(0, 0), 0, n, k // NC)
                    n += 1
                if k == NC - 1:
                    prepare(Batch(1, 0))

            def emit(B, prev, nxt, prep):
                u, n = ring_start(B.b), 0
                for k in range(STEPS):
                    if nxt:
                        maxima(B.plus(1), u, n, k)
                        n += NC
                    if k == 1 and prep:
                        stats1(B.plus(3))
                    if k == 1 and prev:
                        divide(B.plus(-1))
                    if k == 2 and prep:
                        norm1(B.plus(3))
                    if k == 3 and nxt:
                        split_maxima(B.plus(1), u, n, 0)
                        n += 1
                    if k == 3 and prev:
                        stats2(B.plus(-1))
                    if k == 4 and prev:
                        norm2(B.plus(-1))
                    if k == 5 and prev:
                        take_xt(B.plus(-1), u, n)
                        n += 1
                    if k == 6 and prev:
                        choose(B.plus(-1), u, n)
                        n += 1
                    if k == 7 and prev:
                        rank(B.plus(-1), u, n)
                        n += 2
                    if k == 7 and nxt:
                        split_maxima(B.plus(1), u, n, 1)

            rounds(dve, emit, lambda: (chain, chain.n, DVE_BATCH))
            last, u = Batch(7, 1), ring_start(NB - 1) + 4
            divide(last)
            stats2(last)
            norm2(last)
            take_xt(last, u, 0)
            choose(last, u, 1)
            rank(last, u, 2)
            u += 4

            dve.wait_ge(ring_free, u)
            for step in (
                lambda: nc.vector.scalar_tensor_tensor(counts_n[:], expert_iota[:], -float(CAP), count[:], ALU.mult, ALU.add),
                lambda: nc.vector.tensor_tensor(fill[:], counts_n[:].unsqueeze(2).to_broadcast([128, NE, NB]),
                                                block_iota[:], ALU.is_gt),
                lambda: nc.vector.reduce_sum(tiles[:], fill[:], AX.X),
                lambda: nc.vector.tensor_tensor(tri[:], up_to[:], tiles[:].unsqueeze(1).to_broadcast([128, NE, NE]),
                                                ALU.mult),
                lambda: nc.vector.reduce_sum(ends[:], tri[:], AX.X),
                lambda: nc.vector.tensor_scalar(passed[:], ends[:], slot_iota[:], None, ALU.is_le),
                lambda: nc.vector.reduce_sum(slot_f[:, 0:1], passed[:], AX.X),
                lambda: nc.vector.tensor_tensor(passed[:], passed[:], tiles[:], ALU.mult),
                lambda: nc.vector.reduce_sum(slot_f[:, 1:2], passed[:], AX.X),
                lambda: nc.vector.scalar_tensor_tensor(slot_f[:, 2:3], slot_f[:, 0:1], float(CAP // 128), slot_iota[:],
                                                       ALU.mult, ALU.add),
                lambda: nc.vector.tensor_tensor(slot_f[:, 2:3], slot_f[:, 2:3], slot_f[:, 1:2], ALU.subtract),
                lambda: nc.vector.tensor_scalar(slot_f[:, 3:4], slot_f[:, 0:1], float(NE - 1), None, ALU.min),
            ):
                chain.add(step())
                chain.settle()
            nc.vector.tensor_copy(slot_block[:], slot_f[:, 2:3]).then_inc(slots_ready, 1)
            dve.wait_ge(ring_full, u + 1)
            nc.vector.tensor_copy(slot_expert[:], ps_ring[0:1, 0, 0:128]).then_inc(expert_ready, 1)
            dve.wait_ge(tokens_in, 16)
            nc.vector.tensor_copy(slot_tokens_f[:], slot_tokens[:]).then_inc(tokens_f, 1)
            dve.wait_ge(ring_full, u + 2)
            nc.vector.tensor_copy(token_cols[:], ps_ring[:, 1, 0:32]).then_inc(cols_ready, 1)
            dve.wait_ge(bias_in, 16)
            dve.wait_ge(expert_ready, 1)

            def combine(s, i, r):
                e = nc.vector.value_load(slot_expert[0:1, bass.ds(s, 1)],
                                         min_val=0, max_val=NE - 1)
                dve.wait_ge(y_full, s + 1)
                nc.vector.tensor_tensor(y_sum[r % 2], ps_y[:, r % 2],
                                        bias_sb[:, bass.ds(e, 1)].rearrange("p o n -> p (o n)"), ALU.add).then_inc(y_read, 1)
                dve.wait_ge(y_read, s + 1)
                wait(dve, y_stored[r], i * 16)
                nc.vector.scalar_tensor_tensor(y_out[r], y_sum[r % 2], recs_in[r][:, 2 * DM:2 * DM + 1],
                                               recs_in[r][:, DM:2 * DM], ALU.mult, ALU.add).then_inc(y_ready, 1)

            for r in range(NREC):
                combine(r, 0, r)
            with dve.Fori(1, NSLOT // NREC) as i:
                for r in range(NREC):
                    combine(i * NREC + r, i, r)
            for s in range(NSLOT // NREC * NREC, NSLOT):
                combine(s, s // NREC, s % NREC)

        @block.tensor
        def _(pe):
            def scores_for_max(B, u, n, k):
                g, j = divmod(k, NJ)
                if j == 0:
                    pe.wait_ge(stack_in[B.p][g], B.i * (16 * 9) + 16 * 9)
                for c in range(NC):
                    wait(pe, ring_free, u + (n + c - 1))
                    nc.tensor.matmul(ps_ring[:, (n + c) % 2], q_stack[0:KS, B.p, g, j, c * 128:(c + 1) * 128],
                                     k_stack[0:KS, B.p, g, j], start=True, stop=True).then_inc(ring_full, 1)

            def turn_maxima(B, u, n, g):
                pe.wait_ge(ring_free, u + n)
                nc.tensor.transpose(ps_ring[0:NJ * NC, n % 2, 0:128], neg_max[:, g].rearrange("p j c -> p (j c)"),
                                    identity[:]).then_inc(ring_full, 1)

            def scores(B, k):
                g, c = divmod(k, NC)
                if c == 0:
                    pe.wait_ge(shift_in[g], B.b * 48 + 48)
                for jp in range(2):
                    wait(pe, exp_done, B.b * (2 * STEPS) + (2 * k + jp - 1))
                    for j in (2 * jp, 2 * jp + 1):
                        last = nc.tensor.matmul(ps_scores[:, jp, j % 2], k_stack[0:KA, B.p, g, j, c * 128:(c + 1) * 128],
                                                q_stack[0:KA, B.p, g, j], start=True, stop=True)
                    last.then_inc(scores_ready, 1)

            def values(B, k):
                g, c = divmod(k, NC)
                pe.wait_ge(exp_done, B.b * (2 * STEPS) + (2 * k + 2))
                if k == 0:
                    pe.wait_ge(v_ready, B.b + 1)
                if c == 0:
                    wait(pe, (low_read, high_read)[g], B.b * 2)
                for j in range(NJ):
                    last = nc.tensor.matmul(ps_pv[32 * j:32 * j + 32, g], v_ones[:, B.p, c, g, j], probs[:, k % 2, j],
                                            start=c == 0, stop=c == NC - 1)
                last.then_inc(pv_done, 1)

            def turn_rows(B, u, n):
                pe.wait_ge(xn2_ready, B.b + 1)
                pe.wait_ge(ring_free, u + (n - 1))
                for c in range(NC):
                    last = nc.tensor.transpose(ps_ring[:, n % 2, c * 128:(c + 1) * 128], rec[:, c * 128:(c + 1) * 128],
                                               identity[:])
                last.then_inc(ring_full, 1)

            def route(B, u, n):
                pe.wait_ge(ring_free, u + n)
                for c in range(NC):
                    last = nc.tensor.matmul(ps_ring[:, n % 2, 0:NE], xt[:, 0, c], wg_sb[:, c], start=c == 0,
                                            stop=c == NC - 1)
                last.then_inc(ring_full, 1)

            def rank(B, u, n):
                pe.wait_ge(onehot_ready, B.b + 1)
                for m, left in enumerate((before, ones_bf)):
                    pe.wait_ge(ring_free, u + (n + m - 1))
                    nc.tensor.matmul(ps_ring[:, (n + m) % 2, 0:NE], left[:], onehot[:], start=True,
                                     stop=True).then_inc(ring_full, 1)

            pe.wait_ge(pool_const, POOL_CONSTS)
            pe.wait_ge(dve_const, DVE_CONSTS)
            pe.wait_ge(consts_in, 16 * 3)
            n = 0
            for k in range(STEPS):
                scores_for_max(Batch(0, 0), 0, n, k)
                n += NC
                if k % NC == NC - 1:
                    turn_maxima(Batch(0, 0), 0, n, k // NC)
                    n += 1

            def emit(B, prev, nxt, prep):
                u, n = ring_start(B.b), 0
                for k in range(STEPS):
                    scores(B, k)
                    if nxt:
                        scores_for_max(B.plus(1), u, n, k)
                        n += NC
                    if k > 0:
                        values(B, k - 1)
                    elif prev:
                        values(B.plus(-1), STEPS - 1)
                    if k == 3 and nxt:
                        turn_maxima(B.plus(1), u, n, 0)
                        n += 1
                    if k == 5 and prev:
                        turn_rows(B.plus(-1), u, n)
                        n += 1
                    if k == 6 and prev:
                        route(B.plus(-1), u, n)
                        n += 1
                    if k == 7 and prev:
                        rank(B.plus(-1), u, n)
                        n += 2
                    if k == 7 and nxt:
                        turn_maxima(B.plus(1), u, n, 1)

            rounds(pe, emit)
            last, u = Batch(7, 1), ring_start(NB - 1) + 4
            values(last, STEPS - 1)
            turn_rows(last, u, 0)
            route(last, u, 1)
            rank(last, u, 2)
            u += 4
            pe.wait_ge(slots_ready, 1)
            pe.wait_ge(ring_free, u)
            nc.tensor.transpose(ps_ring[0:1, 0, 0:128], slot_f[:, 3:4], identity[:]).then_inc(ring_full, 1)
            pe.wait_ge(tokens_f, 1)
            nc.tensor.transpose(ps_ring[:, 1, 0:32], slot_tokens_f[:], identity[0:32, 0:32]).then_inc(ring_full, 1)
            pe.wait_ge(expert_ready, 1)
            pe.wait_ge(w_loaded, 16 * NB)

            def turn_slot(s, i, r):
                pe.wait_ge(rec_in[r], i * 16 + 16)
                wait(pe, f_xt_ready, s - 1)
                for c in range(NC):
                    last = nc.tensor.transpose(ps_xt[:, r % 2, c * 128:(c + 1) * 128], recs_in[r][:, c * 128:(c + 1) * 128],
                                               identity[:])
                last.then_inc(f_xt_full, 1)

            def expert(s, r):
                e = nc.tensor.value_load(slot_expert[0:1, bass.ds(s, 1)],
                                         min_val=0, max_val=NE - 1)
                pe.wait_ge(f_xt_ready, s + 1)
                wait(pe, y_read, s - 1)
                for c in range(NC):
                    last = nc.tensor.matmul(ps_y[:, r % 2], xt[:, r % 2, c],
                                            w_sb[:, c, bass.ds(e, 1)].rearrange("p o n -> p (o n)"),
                                            start=c == 0, stop=c == NC - 1)
                last.then_inc(y_full, 1)

            turn_slot(0, 0, 0)
            for r in range(NREC):
                turn_slot(r + 1, (r + 1) // NREC, (r + 1) % NREC)
                expert(r, r)
            with pe.Fori(1, (NSLOT - 1) // NREC) as i:
                for r in range(NREC):
                    turn_slot(i * NREC + (r + 1), i + (r + 1) // NREC, (r + 1) % NREC)
                    expert(i * NREC + r, r)
            for s in range((NSLOT - 1) // NREC * NREC, NSLOT):
                if s + 1 < NSLOT:
                    turn_slot(s + 1, (s + 1) // NREC, (s + 1) % NREC)
                expert(s, s % NREC)


def kernel(x, ctx_2048, g_xattn, g_ffn, L0_ffn_wg, L0_ffn_W, L0_ffn_b):
    import numpy as np
    import concourse.bacc as bacc
    from concourse import mybir as mb
    from concourse.bass_utils import run_bass_kernel_spmd as run

    x = np.ascontiguousarray(x)
    c = np.ascontiguousarray(ctx_2048)

    def feature_first(a):
        return a.reshape(NB, NJ, NG, DH, DM).transpose(0, 3, 2, 1, 4).reshape(NB, ROWS, DM)

    arrays = {
        "x_rows": x,
        "x_perm": feature_first(x),
        "k_perm": feature_first(c),
        "v_t": c.reshape(NB, NJ, NG, DH, NC, 128).transpose(0, 5, 4, 2, 1, 3).reshape(NB, 128, DM),
        "w_t": np.asarray(L0_ffn_W).transpose(2, 0, 1).reshape(NC, 128, NE * DM).transpose(1, 0, 2)
               .reshape(128, NB, NC * NE * DM // NB).transpose(1, 0, 2),
        "wg_t": np.asarray(L0_ffn_wg).reshape(NC, 128, NE).transpose(1, 0, 2).reshape(128, NC * NE),
        "bias": np.asarray(L0_ffn_b).reshape(NE * DM),
        "g_attn": np.asarray(g_xattn).reshape(1),
        "g_ffn": np.asarray(g_ffn).reshape(1),
    }
    arrays = {name: np.ascontiguousarray(a) for name, a in arrays.items()}
    nc = bacc.Bacc("TRN2", target_bir_lowering=False, num_devices=1)
    args = {name: nc.dram_tensor(name, a.shape, mb.dt.from_np(a.dtype), kind="ExternalInput").ap()
            for name, a in arrays.items()}
    out = nc.dram_tensor("out", [NT, DM], F32, kind="ExternalOutput").ap()
    build(nc, out=out, **args)
    r = run(nc, [arrays], core_ids=[0])
    return r.results[0]["out"].reshape(NB, ROWS, DM)
```

```python
import concourse.bass as bass
from concourse import mybir
from contextlib import ExitStack

F32, BF16, I32, U32 = mybir.dt.float32, mybir.dt.bfloat16, mybir.dt.int32, mybir.dt.uint32
ALU = mybir.AluOpType
ACT = mybir.ActivationFunctionType
AX = mybir.AxisListType

NB, ROWS, DM = 16, 128, 512
NH, DH = 8, 16
NG, NJ = 2, 4
NC = DM // 128
STEPS = NG * NC
NP = 3
TERMS = 6
KS = TERMS * DH
KA = 128
EPS = 1e-5
NE = 8
NT = NB * ROWS
CAP = NT
NSLOT = NT // 128 + NE - 1
NONE = 2 * NT
REC = 2 * DM + 4
NREC = 4
QTERM = [0, 0, 0, 1, 1, 2]
RING_FIRST, RING_BATCH = 34, 37
DVE_BATCH, POOL_BATCH = 17, 11


class Batch:

    def __init__(self, i, p):
        self.i, self.p = i + p // 2, p % 2
        self.b = self.i * 2 + self.p

    def plus(self, n):
        return Batch(self.i, self.p + n) if n >= 0 else Batch(self.i - 1, self.p + n + 2)


class Chain:

    def __init__(self, eng, sem):
        self.eng, self.sem, self.base, self.n = eng, sem, 0, 0

    def add(self, op):
        op.then_inc(self.sem, 1)
        self.n += 1

    def settle(self):
        self.eng.wait_ge(self.sem, self.base + self.n)


def wait(eng, sem, value):
    if not isinstance(value, int) or value > 0:
        eng.wait_ge(sem, value)


def stand_alone(eng):
    eng.nop(nofuse=True)


class Turns:

    def __init__(self, B, ahead, rows):
        if isinstance(B.b, int) and B.b == 0:
            self.full0 = self.read0 = self.odd = RING_FIRST
        else:
            self.full0 = B.b * RING_BATCH + (2 * RING_FIRST - RING_BATCH)
            self.read0 = B.b * (RING_BATCH - 1) + (2 * RING_FIRST - RING_BATCH + 1)
            self.odd = B.p * RING_BATCH + RING_BATCH
        self.rows_at = (6 * NC + 1 if ahead else 0) if rows else None

    def slot(self, n):
        return (self.odd + n) % 2

    def fulls(self, n):
        return self.full0 + n

    def reads(self, n):
        return self.read0 + (n - (self.rows_at is not None and n > self.rows_at))


def build(nc, x_rows, x_perm, k_perm, v_t, w_t, wg_t, bias, g_attn, g_ffn, out):
    ctx = ExitStack()
    with ctx:
        def sb(name, shape, dt=F32):
            return ctx.enter_context(nc.sbuf_tensor(name, shape, dt))

        def sem(name):
            return ctx.enter_context(nc.semaphore(name))

        parts_dram = nc.dram_tensor("parts_dram", [NB, 2, NP, ROWS, DM], BF16, kind="Internal").ap()
        recs_dram = nc.dram_tensor("recs_dram", [NT, REC], F32, kind="Internal").ap()
        table_dram = nc.dram_tensor("table_dram", [NE * CAP, 1], I32, kind="Internal").ap()
        table_blocks = table_dram.rearrange("(k p) o -> k (p o)", p=128)

        identity = sb("identity", [128, 128])
        earlier = sb("earlier", [128, 128], BF16)
        ones_bf = sb("ones_bf", [128, 128], BF16)
        low_half = sb("low_half", [128, 1])
        high_half = sb("high_half", [128, 1])
        gates = sb("gates", [128, 4])
        low_gate = sb("low_gate", [128, 1])
        high_gate = sb("high_gate", [128, 1])
        power = sb("power", [128, 1])
        minus = sb("minus", [128, 1])
        expert_iota = sb("expert_iota", [128, NE])
        block_iota = sb("block_iota", [128, NE, NB])
        up_to = sb("up_to", [128, NE, NE])
        slot_iota = sb("slot_iota", [128, 1])
        zeros = sb("zeros", [NP, NJ * DM], BF16)
        mark = sb("mark", [1, 1])
        none_i = sb("none_i", [128, 128], I32)
        wg_sb = sb("wg_sb", [128, NC, NE])
        w_sb = sb("w_sb", [128, NC, NE, DM])
        xp_in = sb("xp_in", [128, DM])
        k_in = sb("k_in", [128, DM])
        v_in = sb("v_in", [128, NC, NG, NJ, DH])
        x_in = sb("x_in", [128, DM])
        qn = sb("qn", [128, DM])
        resid = sb("resid", [128, 2, DM])
        parts = sb("parts", [128, 2, NP, DM], BF16)
        q_stack = sb("q_stack", [128, 2, NG, NJ, DM], BF16)
        k_stack = sb("k_stack", [128, 2, NG, NJ, DM], BF16)
        v_ones = sb("v_ones", [128, 2, NC, NG, NJ, 2 * DH])
        neg_max = sb("neg_max", [128, NG, NJ, NC])
        shift_rest = sb("shift_rest", [NJ * NC, NG, 128])
        shift_parts = sb("shift_parts", [NJ * NC, NG, NP, 128], BF16)
        probs = sb("probs", [128, 2, NJ, DM])
        low_num = sb("low_num", [128, DM])
        high_num = sb("high_num", [128, DM])
        num = sb("num", [128, DM])
        den = sb("den", [128, DM])
        den_turned = sb("den_turned", [128, NG, DM])
        recip = sb("recip", [128, NG, DM // 32])
        recip_turned = sb("recip_turned", [128, DM])
        rec = sb("rec", [128, REC])
        xt = sb("xt", [128, 2, NC, 128])
        st1 = sb("st1", [128, 6])
        mv1 = sb("mv1", [128, 2])
        rs1 = sb("rs1", [128, 3])
        st2 = sb("st2", [128, 6])
        mv2 = sb("mv2", [128, 2])
        rs2 = sb("rs2", [128, 3])
        logits = sb("logits", [128, NE])
        top = sb("top", [128, 8])
        top_at = sb("top_at", [128, 8], U32)
        top_f = sb("top_f", [128, 1])
        neg_top = sb("neg_top", [128, 1])
        gate_exp = sb("gate_exp", [128, NE])
        gate_sum = sb("gate_sum", [128, 1])
        gate_inv = sb("gate_inv", [128, 1])
        onehot = sb("onehot", [128, NE], BF16)
        place = sb("place", [128, NE])
        dest_f = sb("dest_f", [128, 1])
        dest_i = sb("dest_i", [128, 1], I32)
        token_f = sb("token_f", [128, 1])
        token_i = sb("token_i", [128, 1], I32)
        count = sb("count", [128, NE])
        ffn_rec = k_stack[:].rearrange("p a g j m -> p (a g j m)").bitcast(F32)
        q_flat = q_stack[:].rearrange("p a g j m -> p (a g j m)").bitcast(F32)
        bias_sb = q_flat[:, 0:NE * DM].rearrange("p (e n) -> p e n", e=NE)
        rec_buf = sb("rec_buf", [128, REC])
        recs_in = [probs[:].rearrange("p a j m -> p (a j m)")[:, r * REC:(r + 1) * REC] for r in range(3)]
        recs_in.append(rec_buf[:])
        y_sum = [v_ones[:].rearrange("p a c g j d -> p (a c g j d)")[:, r * DM:(r + 1) * DM] for r in range(2)]
        y_out = [ffn_rec[:, r * DM:(r + 1) * DM] for r in range(NREC)]
        counts_n = sb("counts_n", [128, NE])
        fill = sb("fill", [128, NE, NB])
        tiles = sb("tiles", [128, NE])
        tri = sb("tri", [128, NE, NE])
        ends = sb("ends", [128, NE])
        passed = sb("passed", [128, NE])
        slot_f = sb("slot_f", [128, 4])
        slot_block = sb("slot_block", [128, 1], I32)
        slot_expert = sb("slot_expert", [1, 128], I32)
        slot_tokens = sb("slot_tokens", [32, 128], I32)
        slot_tokens_f = sb("slot_tokens_f", [32, 128])
        token_cols = sb("token_cols", [128, 32], I32)

        ps_scores = ctx.enter_context(nc.psum_tensor("ps_scores", [128, 2, 2, DM], F32))
        ps_ring = ctx.enter_context(nc.psum_tensor("ps_ring", [128, 2, DM], F32))
        ps_pv = ctx.enter_context(nc.psum_tensor("ps_pv", [128, NG, DM], F32))
        ps_y = ps_scores[:, 0]
        ps_xt = ps_scores[:, 1]

        consts_in = sem("consts_in")
        table_set = sem("table_set")
        xk_in = sem("xk_in")
        v_loaded = sem("v_loaded")
        x_loaded = sem("x_loaded")
        w_loaded = sem("w_loaded")
        parts_out = sem("parts_out")
        stack_in = [[sem(f"stack_in{p}{g}") for g in range(NG)] for p in range(2)]
        shift_in = [sem(f"shift_in{g}") for g in range(NG)]
        rec_out = sem("rec_out")
        table_out = sem("table_out")
        pool_const = sem("pool_const")
        dve_const = sem("dve_const")
        gates_ready = sem("gates_ready")
        ln1_stats, ln1_rstd, qn_ready = sem("ln1_stats"), sem("ln1_rstd"), sem("qn_ready")
        high_cast, mid_cast = sem("high_cast"), sem("mid_cast")
        rest_ready, low_ready = sem("rest_ready"), sem("low_ready")
        v_ready = sem("v_ready")
        ring_full, ring_free = sem("ring_full"), sem("ring_free")
        rows_taken = sem("rows_taken")
        shift_ready = sem("shift_ready")
        scores_ready, exp_done, pv_done = sem("scores_ready"), sem("exp_done"), sem("pv_done")
        low_read, high_read = sem("low_read"), sem("high_read")
        low_turned, high_turned = sem("low_turned"), sem("high_turned")
        shift_rest_ready = sem("shift_rest_ready")
        recip_ready, x1_done = sem("recip_ready"), sem("x1_done")
        ln2_stats, ln2_rstd, xn2_ready = sem("ln2_stats"), sem("ln2_rstd"), sem("xn2_ready")
        top_ready, gate_summed = sem("top_ready"), sem("gate_summed")
        onehot_ready, dest_ready, gate_ready = sem("onehot_ready"), sem("dest_ready"), sem("gate_ready")
        dve_chain, pool_chain = sem("dve_chain"), sem("pool_chain")
        bias_in = sem("bias_in")
        slots_ready, expert_ready = sem("slots_ready"), sem("expert_ready")
        tokens_in, tokens_f, cols_ready = sem("tokens_in"), sem("tokens_f"), sem("cols_ready")
        rec_in = [sem(f"rec_in{r}") for r in range(NREC)]
        f_xt_full, f_xt_ready = sem("f_xt_full"), sem("f_xt_ready")
        y_full, y_read, y_ready = sem("y_full"), sem("y_read"), sem("y_ready")
        y_stored = [sem(f"y_stored{r}") for r in range(NREC)]

        DVE_CONSTS = 18
        POOL_CONSTS = 13
        block = ctx.enter_context(nc.Block())

        start_turns, end_turns = Turns(Batch(0, 0), True, False), Turns(Batch(7, 1), False, True)
        start_turns.full0 = start_turns.read0 = start_turns.odd = 0
        end_turns.full0, end_turns.read0 = end_turns.fulls(3), end_turns.reads(3)
        end_turns.odd += 3

        def rounds(eng, emit, after_first=None):
            for n in range(2):
                emit(Batch(n // 2, n % 2), n > 0, False, True, True)
            start = after_first() if after_first else None
            with eng.Fori(1, 6) as i:
                for p in range(2):
                    B = Batch(i, p)
                    if start is not None:
                        start[0].base, start[0].n = (i - 1) * (2 * start[2]) + (start[1] + p * start[2]), 0
                    emit(B, True, True, True, True)
                    if start is not None:
                        assert start[0].n == start[2], (start[0].n, start[2])
            if start is not None:
                start[0].base, start[0].n = start[1] + 10 * start[2], 0
            for n in range(12, NB):
                emit(Batch(n // 2, n % 2), True, True, n + 1 < NB, n + 3 < NB)

        @block.sync
        def _(sp):
            def load_rows_keys(B):
                wait(sp, rest_ready, B.b * 2)
                if not isinstance(B.b, int):
                    stand_alone(sp)
                sp.dma_start(xp_in[:], x_perm[bass.ds(B.b, 1)].rearrange("o p m -> (o p) m")).then_inc(xk_in, 16)
                sp.dma_start(k_in[:], k_perm[bass.ds(B.b, 1)].rearrange("o p m -> (o p) m")).then_inc(xk_in, 16)

            def load_values(B):
                wait(sp, v_ready, B.b)
                if not isinstance(B.b, int):
                    stand_alone(sp)
                sp.dma_start(v_in[:].rearrange("p c g j d -> p (c g j d)"),
                             v_t[bass.ds(B.b, 1)].rearrange("o p m -> (o p) m")).then_inc(v_loaded, 16)

            def load_residual(B):
                wait(sp, x1_done, B.b)
                if not isinstance(B.b, int):
                    stand_alone(sp)
                sp.dma_start(x_in[:], x_rows[bass.ds(B.b, 1)].rearrange("o p m -> (o p) m")).then_inc(x_loaded, 16)

            def load_stack(B, g):
                wait(sp, parts_out, B.b * 16 + 16)
                if not isinstance(B.b, int):
                    stand_alone(sp)
                wait(sp, scores_ready, B.b * (2 * STEPS) + (STEPS * (g + 1) - 4 * STEPS))
                if not isinstance(B.b, int):
                    stand_alone(sp)
                mine = parts_dram[bass.ds(B.b, 1)].rearrange("o s t (c g j) m -> s (o g) t c (j m)", g=NG, j=NJ)
                for n, t in enumerate(QTERM):
                    sp.dma_start(q_stack[n * DH:(n + 1) * DH, B.p, g].rearrange("p j m -> p (j m)"),
                                 mine[0, g, t]).then_inc(stack_in[B.p][g], 16)
                sp.dma_start(q_stack[KS:KS + NP, B.p, g].rearrange("p j m -> p (j m)"),
                             zeros[:]).then_inc(stack_in[B.p][g], 16)
                for first, n in ((0, 3), (3, 2), (5, 1)):
                    sp.dma_start(k_stack[first * DH:(first + n) * DH, B.p, g].rearrange("p j m -> p (j m)"),
                                 mine[1, g, 0:n].rearrange("t c m -> (t c) m")).then_inc(stack_in[B.p][g], 16)

            def load_shift(B, g):
                sp.wait_ge(shift_ready, B.b * 2 + (g + 1))
                for t in range(NP):
                    sp.dma_start(q_stack[KS + t:KS + t + 1, B.p, g].rearrange("o j (c m) -> o (j c) m", c=NC),
                                 shift_parts[:, g, t]).then_inc(shift_in[g], 16)

            def load_weights(B):
                n = NC * NE * DM // NB
                sp.dma_start(w_sb[:].rearrange("p c e n -> p (c e n)")[:, bass.ds(B.b * n, n)],
                             w_t[bass.ds(B.b, 1)].rearrange("o p n -> (o p) n")).then_inc(w_loaded, 16)

            def store_record(B):
                sp.wait_ge(gate_ready, B.b + 1)
                stand_alone(sp)
                sp.dma_start(recs_dram[bass.ds(B.b * ROWS, ROWS)], rec[:]).then_inc(rec_out, 16)

            load_rows_keys(Batch(0, 0))
            sp.dma_start(gates[:, 0:1], g_attn.partition_broadcast(128)).then_inc(consts_in, 16)
            sp.dma_start(gates[:, 1:2], g_ffn.partition_broadcast(128)).then_inc(consts_in, 16)
            sp.dma_start(wg_sb[:].rearrange("p c e -> p (c e)"), wg_t).then_inc(consts_in, 16)
            load_values(Batch(0, 0))
            load_rows_keys(Batch(0, 1))
            sp.wait_ge(dve_const, DVE_CONSTS)
            for g in range(NG):
                load_stack(Batch(0, 0), g)
            load_rows_keys(Batch(1, 0))
            for g in range(NG):
                load_stack(Batch(0, 1), g)
            for g in range(NG):
                load_shift(Batch(0, 0), g)
            sp.wait_ge(pool_const, POOL_CONSTS)
            sp.dma_start(table_dram.rearrange("(k p) o -> k (p o)", p=128), none_i[:]).then_inc(table_set, 16)
            load_values(Batch(0, 1))

            def emit(B, prev, prev2, nxt, prep):
                if prep:
                    load_rows_keys(B.plus(3))
                if prev2:
                    store_record(B.plus(-2))
                load_weights(B)
                stack = not isinstance(B.b, int) or B.b + 2 < NB
                if stack:
                    load_stack(B.plus(2), 0)
                    load_values(B.plus(2))
                load_residual(B)
                if nxt:
                    load_shift(B.plus(1), 0)
                if stack:
                    load_stack(B.plus(2), 1)
                if nxt:
                    load_shift(B.plus(1), 1)

            rounds(sp, emit)
            store_record(Batch(7, 0))
            sp.wait_ge(scores_ready, 2 * STEPS * NB)
            sp.dma_start(bias_sb.rearrange("p e n -> p (e n)"), bias.partition_broadcast(128)).then_inc(bias_in, 16)
            store_record(Batch(7, 1))

        @block.gpsimd
        def _(pool):
            chain = Chain(pool, pool_chain)
            steps = [lambda: nc.gpsimd.memset(identity[:], 0.0),
                     lambda: nc.gpsimd.affine_select(out=identity[:], in_=identity[:], compare_op=ALU.not_equal, fill=1.0,
                                                     base=0, pattern=[[-1, 128]], channel_multiplier=1),
                     lambda: nc.gpsimd.memset(earlier[:], 1.0),
                     lambda: nc.gpsimd.affine_select(out=earlier[:], in_=earlier[:], compare_op=ALU.is_gt, fill=0.0,
                                                     base=0, pattern=[[1, 128]], channel_multiplier=-1),
                     lambda: nc.gpsimd.memset(ones_bf[:], 1.0),
                     lambda: nc.gpsimd.memset(power[:], -0.5),
                     lambda: nc.gpsimd.memset(minus[:], -1.0),
                     lambda: nc.gpsimd.iota(none_i[:], [[0, 128]], base=NONE, channel_multiplier=0),
                     lambda: nc.gpsimd.iota(expert_iota[:], [[1, NE]], base=0, channel_multiplier=0,
                                            allow_small_or_imprecise_dtypes=True),
                     lambda: nc.gpsimd.iota(block_iota[:], [[0, NE], [128, NB]], base=0, channel_multiplier=0,
                                            allow_small_or_imprecise_dtypes=True),
                     lambda: nc.gpsimd.iota(slot_iota[:], [[0, 1]], base=0, channel_multiplier=1,
                                            allow_small_or_imprecise_dtypes=True),
                     lambda: nc.gpsimd.iota(token_f[:], [[0, 1]], base=0, channel_multiplier=1,
                                            allow_small_or_imprecise_dtypes=True),
                     lambda: nc.gpsimd.iota(count[:], [[CAP, NE]], base=0, channel_multiplier=0,
                                            allow_small_or_imprecise_dtypes=True)]
            assert len(steps) == POOL_CONSTS
            for n, step in enumerate(steps):
                step().then_inc(pool_const, 1)
                pool.wait_ge(pool_const, n + 1)

            def rstd(B, stats, mv, rs, done, scale):
                pool.wait_ge(stats, B.b + 1)
                stand_alone(pool)
                chain.add(nc.gpsimd.tensor_scalar(rs[:, 0:1], mv[:, 1:2], EPS, scale, ALU.add, ALU.mult))
                chain.settle()
                chain.add(nc.gpsimd.tensor_tensor(rs[:, 1:2], rs[:, 0:1], power[:], ALU.pow))
                chain.settle()
                chain.add(nc.gpsimd.tensor_tensor(rs[:, 0:1], rs[:, 1:2], mv[:, 0:1], ALU.mult))
                chain.settle()
                nc.gpsimd.tensor_tensor(rs[:, 2:3], rs[:, 0:1], minus[:], ALU.mult).then_inc(done, 1)

            def rstd1(B):
                wait(pool, qn_ready, B.b)
                rstd(B, ln1_stats, mv1, rs1, ln1_rstd, float(DH))

            def rstd2(B):
                wait(pool, xn2_ready, B.b)
                rstd(B, ln2_stats, mv2, rs2, ln2_rstd, 1.0)

            def copy_values(B):
                pool.wait_ge(v_loaded, B.b * 16 + 16)
                wait(pool, pv_done, (B.b - 1) * STEPS)
                stand_alone(pool)
                chain.add(nc.gpsimd.tensor_copy(v_ones[:, B.p, :, 0, :, 0:DH], v_in[:, :, 0]))
                nc.gpsimd.tensor_copy(v_ones[:, B.p, :, 1, :, DH:2 * DH], v_in[:, :, 1]).then_inc(v_ready, 1)

            def rests(B):
                for s, src in enumerate((qn, k_in)):
                    pool.wait_ge(high_cast, B.b * 2 + (s + 1))
                    wait(pool, low_ready, B.b * 2)
                    nc.gpsimd.tensor_tensor(resid[:, s], src[:], parts[:, s, 0], ALU.subtract).then_inc(rest_ready, 1)

            def lows(B):
                for s in range(2):
                    pool.wait_ge(mid_cast, B.b * 2 + (s + 1))
                    nc.gpsimd.tensor_tensor(parts[:, s, 2], resid[:, s], parts[:, s, 1], ALU.subtract).then_inc(low_ready, 1)
                pool.wait_ge(low_ready, B.b * 2 + 2)
                pool.dma_start(parts_dram[bass.ds(B.b, 1)].rearrange("o s t p m -> p (o s t) m"),
                               parts[:].rearrange("p s t m -> p (s t) m")).then_inc(parts_out, 16)

            def add_attention(B):
                pool.wait_ge(high_read, B.b + 1)
                chain.add(nc.gpsimd.tensor_tensor(num[:], low_num[:], high_num[:], ALU.add))
                chain.settle()
                pool.wait_ge(recip_ready, B.b + 1)
                pool.wait_ge(x_loaded, B.b * 16 + 16)
                wait(pool, rec_out, B.b * 16)
                chain.add(nc.gpsimd.tensor_tensor(num[:], num[:], den[:], ALU.mult))
                chain.settle()
                nc.gpsimd.tensor_tensor(rec[:, DM:2 * DM], num[:], x_in[:], ALU.add).then_inc(x1_done, 1)

            def split_rest(B, g):
                pool.wait_ge(shift_rest_ready, B.b * 2 + (g + 1))
                stand_alone(pool)
                chain.add(nc.gpsimd.tensor_copy(shift_parts[:, g, 1], shift_rest[:, g]))
                chain.settle()
                nc.gpsimd.tensor_tensor(shift_parts[:, g, 2], shift_rest[:, g], shift_parts[:, g, 1],
                                        ALU.subtract).then_inc(shift_ready, 1)

            def store_tokens(B):
                pool.wait_ge(dest_ready, B.b + 1)
                stand_alone(pool)
                if isinstance(B.b, int) and B.b == 0:
                    pool.wait_ge(table_set, 16)
                pool.indirect_dma_start(table_dram, bass.IndirectOffsetOnAxis(ap=dest_i[:, 0:1], axis=0),
                                        token_i[:], None).then_inc(table_out, 16)

            for n in range(3):
                B = Batch(n // 2, n % 2)
                rstd1(B)
                rests(B)
                lows(B)
                if n == 0:
                    pool.wait_ge(dve_const, DVE_CONSTS)
                    copy_values(B)
                if n == 1:
                    split_rest(Batch(0, 0), 0)

            def emit(B, prev, prev2, nxt, prep):
                if nxt:
                    copy_values(B.plus(1))
                if prev2:
                    store_tokens(B.plus(-2))
                if prep:
                    rstd1(B.plus(3))
                if prev:
                    add_attention(B.plus(-1))
                if prep:
                    rests(B.plus(3))
                if nxt:
                    split_rest(B.plus(1), 0)
                if prev:
                    rstd2(B.plus(-1))
                if prep:
                    lows(B.plus(3))
                if nxt:
                    split_rest(B.plus(1), 1)

            split_rest(Batch(0, 0), 1)
            rounds(pool, emit, lambda: (chain, chain.n, POOL_BATCH))
            last = Batch(7, 1)
            store_tokens(last.plus(-1))
            add_attention(last)
            rstd2(last)
            store_tokens(last)

            pool.wait_ge(slots_ready, 1)
            pool.wait_ge(table_out, 16 * NB)
            pool.indirect_dma_start(slot_tokens[:], None, table_blocks,
                                    bass.IndirectOffsetOnAxis(ap=slot_block[0:32, 0:1], axis=0),
                                    bounds_check=NE * CAP // 128 - 1, oob_is_err=False).then_inc(tokens_in, 16)
            pool.wait_ge(rec_out, 16 * NB)

            pool.wait_ge(cols_ready, 1)

            def gather(s, r):
                pool.indirect_dma_start(recs_in[r], None, recs_dram,
                                        bass.IndirectOffsetOnAxis(ap=token_cols[:, s:s + 1], axis=0),
                                        bounds_check=NT - 1, oob_is_err=False).then_inc(rec_in[r], 16)

            def scatter(s, r):
                pool.wait_ge(y_ready, s + 1)
                pool.indirect_dma_start(out, bass.IndirectOffsetOnAxis(ap=token_cols[:, s:s + 1], axis=0),
                                        y_out[r], None,
                                        bounds_check=NT - 1, oob_is_err=False).then_inc(y_stored[r], 16)

            for r in range(NREC):
                gather(r, r)
            for s in range(NSLOT):
                scatter(s, s % NREC)
                if s + NREC < NSLOT:
                    gather(s + NREC, s % NREC)
            for r in range(NREC):
                pool.wait_ge(y_stored[r], 16 * len(range(r, NSLOT, NREC)))

        @block.scalar
        def _(act):
            act.wait_ge(consts_in, 16 * 3)
            nc.scalar.activation(gates[:, 2:4], gates[:, 0:2], ACT.Tanh).then_inc(gates_ready, 1)

            def norm1(B):
                act.wait_ge(ln1_rstd, B.b + 1)
                wait(act, rest_ready, B.b * 2)
                nc.scalar.activation(qn[:], xp_in[:], ACT.Identity, bias=rs1[:, 2:3], scale=rs1[:, 1:2]).then_inc(qn_ready, 1)

            def norm2(B):
                act.wait_ge(ln2_rstd, B.b + 1)
                nc.scalar.activation(rec[:, 0:DM], rec[:, DM:2 * DM], ACT.Identity, bias=rs2[:, 2:3],
                                     scale=rs2[:, 1:2]).then_inc(xn2_ready, 1)

            def take_rows(B, u, n):
                act.wait_ge(ring_full, u.fulls(n + 1))
                nc.scalar.copy(xt[:, 0].rearrange("p c n -> p (c n)"), ps_ring[:, u.slot(n)]).then_inc(rows_taken, 1)

            def cast_high(B):
                for s, (src, ready, value) in enumerate(((qn, qn_ready, B.b + 1), (k_in, xk_in, B.b * 32 + 32))):
                    act.wait_ge(ready, value)
                    wait(act, parts_out, B.b * 16)
                    nc.scalar.copy(parts[:, s, 0], src[:]).then_inc(high_cast, 1)

            def cast_mid(B):
                for s in range(2):
                    act.wait_ge(rest_ready, B.b * 2 + (s + 1))
                    nc.scalar.copy(parts[:, s, 1], resid[:, s]).then_inc(mid_cast, 1)

            def read_low(B):
                act.wait_ge(pv_done, B.b * STEPS + NC)
                wait(act, x1_done, B.b)
                nc.scalar.mul(low_num[:], ps_pv[:, 0], low_gate[:]).then_inc(low_read, 1)

            def read_high(B):
                act.wait_ge(high_turned, B.b + 1)
                nc.scalar.mul(high_num[:], ps_pv[:, 1], high_gate[:]).then_inc(high_read, 1)

            def sum_gate(B):
                act.wait_ge(top_ready, B.b + 1)
                nc.scalar.activation(gate_exp[:], logits[:], ACT.Exp, bias=neg_top[:],
                                     accum_out=gate_sum[:]).then_inc(gate_summed, 1)

            def exps(B, k):
                for jp in range(2):
                    act.wait_ge(scores_ready, B.b * (2 * STEPS) + (2 * k + jp + 1))
                    if jp == 0:
                        wait(act, pv_done, B.b * STEPS + (k - 1))
                    nc.scalar.activation(probs[:, k % 2, 2 * jp:2 * jp + 2], ps_scores[:, jp], ACT.Exp).then_inc(exp_done, 1)

            for n in range(3):
                norm1(Batch(n // 2, n % 2))
                cast_high(Batch(n // 2, n % 2))
                cast_mid(Batch(n // 2, n % 2))
                if n == 0:
                    act.wait_ge(dve_const, DVE_CONSTS)

            def emit(B, prev, prev2, nxt, prep):
                for k in range(STEPS):
                    exps(B, k)
                    if k == 1 and prev:
                        read_high(B.plus(-1))
                    if k == 2 and prep:
                        norm1(B.plus(3))
                        cast_high(B.plus(3))
                    if k == 4 and prev:
                        norm2(B.plus(-1))
                    if k == 5 and prev:
                        u = Turns(B, nxt, prev)
                        take_rows(B.plus(-1), u, u.rows_at)
                    if k == 5:
                        read_low(B)
                    if k == 6 and prep:
                        cast_mid(B.plus(3))
                    if k == 7 and prev:
                        sum_gate(B.plus(-1))

            rounds(act, emit)
            read_high(Batch(7, 1))
            norm2(Batch(7, 1))
            take_rows(Batch(7, 1), end_turns, 0)
            sum_gate(Batch(7, 1))

            def evacuate(s, r):
                act.wait_ge(f_xt_full, s + 1)
                wait(act, y_full, s - 1)
                nc.scalar.copy(xt[:, r % 2].rearrange("p c n -> p (c n)"), ps_xt[:, r % 2]).then_inc(f_xt_ready, 1)

            evacuate(0, 0)
            with act.Fori(0, (NSLOT - 1) // 2) as i:
                for r in range(2):
                    evacuate(i * 2 + (r + 1), r + 1)

        @block.vector
        def _(dve):
            chain = Chain(dve, dve_chain)
            steps = [lambda: nc.vector.memset(v_ones[:].rearrange("p a c g j d -> p (a c g j d)"), 1.0),
                     lambda: nc.vector.memset(k_stack[KS:KA].rearrange("p a g j m -> p (a g j m)"), 0.0),
                     lambda: nc.vector.memset(k_stack[KS:KS + NP].rearrange("p a g j m -> p (a g j m)"), 1.0),
                     lambda: nc.vector.memset(q_stack[KS:KA].rearrange("p a g j m -> p (a g j m)"), 0.0),
                     lambda: nc.vector.memset(zeros[:], 0.0),
                     lambda: nc.vector.memset(low_half[:], 0.0)]
            steps += [lambda j=j: nc.vector.memset(low_half[32 * j:32 * j + DH], 1.0) for j in range(NJ)]
            steps += [lambda: nc.vector.tensor_scalar(high_half[:], low_half[:], -1.0, 1.0, ALU.mult, ALU.add),
                      lambda: nc.vector.memset(rec[:, 2 * DM:REC], 0.0),
                      lambda: nc.vector.memset(rec_buf[:], 0.0),
                      lambda: nc.vector.memset(slot_tokens_f[:], float(NONE)),
                      lambda: nc.vector.tensor_copy(slot_tokens[:], slot_tokens_f[:]),
                      lambda: nc.vector.tensor_scalar(low_gate[:], low_half[:], gates[:, 2:3], None, ALU.mult),
                      lambda: nc.vector.tensor_scalar(high_gate[:], high_half[:], gates[:, 2:3], None, ALU.mult),
                      lambda: nc.vector.memset(up_to[:], 0.0)]
            assert len(steps) == DVE_CONSTS
            for n, step in enumerate(steps):
                if n == 15:
                    dve.wait_ge(gates_ready, 1)
                step().then_inc(dve_const, 1)
                dve.wait_ge(dve_const, n + 1)
            for e in range(NE):
                chain.add(nc.vector.memset(up_to[:, e, 0:e + 1], 1.0))
            chain.settle()
            dve.wait_ge(pool_const, POOL_CONSTS)

            def maximum(B, u, n, k, c):
                g, j = divmod(k, NJ)
                dve.wait_ge(ring_full, u.fulls(n + 1))
                nc.vector.tensor_reduce(neg_max[:, g, j, c:c + 1], ps_ring[:, u.slot(n)], AX.X, ALU.max,
                                        negate=True).then_inc(ring_free, 1)

            def split_maxima(B, u, n, g):
                src = ps_ring[0:NJ * NC, u.slot(n), 0:128]
                dve.wait_ge(ring_full, u.fulls(n + 1))
                wait(dve, shift_in[g], B.b * 48)
                chain.add(nc.vector.tensor_copy(shift_parts[:, g, 0], src))
                chain.settle()
                nc.vector.tensor_tensor(shift_rest[:, g], src, shift_parts[:, g, 0], ALU.subtract).then_inc(ring_free, 1)
                dve.wait_ge(ring_free, u.reads(n + 1))
                nc.vector.memset(mark[:], 0.0).then_inc(shift_rest_ready, 1)

            def stats1(B):
                dve.wait_ge(xk_in, B.b * 32 + 32)
                chain.add(nc.vector.bn_stats(st1[:], xp_in[:]))

            def mean1(B):
                chain.settle()
                stand_alone(dve)
                nc.vector.bn_aggr(mv1[:], st1[:]).then_inc(ln1_stats, 1)

            def turn_sums(B, g):
                if g == 0:
                    dve.wait_ge(low_read, B.b + 1)
                else:
                    dve.wait_ge(pv_done, B.b * STEPS + STEPS)
                nc.vector.transpose(den_turned[:, g], ps_pv[:, g]).then_inc((low_turned, high_turned)[g], 1)

            def invert_sums(B, g):
                dve.wait_ge((low_turned, high_turned)[g], B.b + 1)
                at = DH if g == 0 else 0
                chain.add(nc.vector.reciprocal(recip[:, g], den_turned[:, g].rearrange("p (t c) -> p t c", c=32)[:, :, at]))

            def spread_sums(g):
                chain.settle()
                to = 0 if g == 0 else DH
                chain.add(nc.vector.tensor_copy(recip_turned[:].rearrange("p (t c) -> p t c", c=32)[:, :, to:to + DH],
                                                recip[:, g].unsqueeze(2).to_broadcast([128, DM // 32, DH])))

            def turn_back(B):
                chain.settle()
                wait(dve, x1_done, B.b)
                nc.vector.transpose(den[:], recip_turned[:]).then_inc(recip_ready, 1)

            def stats2(B):
                dve.wait_ge(x1_done, B.b + 1)
                chain.add(nc.vector.bn_stats(st2[:], rec[:, DM:2 * DM]))

            def mean2(B):
                chain.settle()
                stand_alone(dve)
                nc.vector.bn_aggr(mv2[:], st2[:]).then_inc(ln2_stats, 1)

            def take_logits(B, u, n):
                dve.wait_ge(ring_full, u.fulls(n + 1))
                nc.vector.tensor_copy(logits[:], ps_ring[:, u.slot(n), 0:NE]).then_inc(ring_free, 1)

            def find_top(B, u, n):
                dve.wait_ge(ring_free, u.reads(n + 1))
                stand_alone(dve)
                chain.add(nc.vector.max(top[:], logits[:]))

            def find_expert(B):
                chain.settle()
                nc.vector.tensor_scalar(neg_top[:], top[:, 0:1], -1.0, None, ALU.mult).then_inc(top_ready, 1)
                chain.add(nc.vector.max_index(top_at[:], top[:], logits[:]))

            def expert_number(B):
                chain.settle()
                chain.add(nc.vector.tensor_copy(top_f[:], top_at[:, 0:1]))

            def mark_expert(B):
                chain.settle()
                nc.vector.tensor_scalar(onehot[:], expert_iota[:], top_f[:], None, ALU.is_equal).then_inc(onehot_ready, 1)

            def take_ranks(B, u, n):
                dve.wait_ge(ring_full, u.fulls(n + 1))
                chain.add(nc.vector.tensor_tensor(place[:], ps_ring[:, u.slot(n), 0:NE], count[:], ALU.add))
                chain.settle()
                nc.vector.tensor_tensor(count[:], count[:], ps_ring[:, u.slot(n), NE:2 * NE], ALU.add).then_inc(ring_free, 1)

            def mask_places(B):
                chain.settle()
                dve.wait_ge(onehot_ready, B.b + 1)
                chain.add(nc.vector.tensor_tensor(place[:], place[:], onehot[:], ALU.mult))

            def sum_places(B):
                chain.settle()
                chain.add(nc.vector.reduce_sum(dest_f[:], place[:], AX.X))

            def number_tokens(B):
                chain.settle()
                wait(dve, table_out, B.b * 16)
                chain.add(nc.vector.tensor_copy(dest_i[:], dest_f[:]))
                chain.add(nc.vector.tensor_copy(token_i[:], token_f[:]))

            def next_tokens(B):
                chain.settle()
                nc.vector.tensor_scalar(token_f[:], token_f[:], float(ROWS), None, ALU.add).then_inc(dest_ready, 1)

            def invert_gate(B):
                dve.wait_ge(gate_summed, B.b + 1)
                chain.add(nc.vector.reciprocal(gate_inv[:], gate_sum[:]))

            def store_gate(B):
                chain.settle()
                nc.vector.tensor_scalar(rec[:, 2 * DM:2 * DM + 1], gate_inv[:], gates[:, 3:4], None,
                                        ALU.mult).then_inc(gate_ready, 1)

            for n in range(2):
                stats1(Batch(0, n))
                mean1(Batch(0, n))
            n = 0
            for k in range(STEPS):
                for c in range(NC):
                    maximum(Batch(0, 0), start_turns, n + c, k, c)
                n += NC
                if k % NC == NC - 1:
                    split_maxima(Batch(0, 0), start_turns, n, k // NC)
                    n += 1
                if k == NC - 1:
                    stats1(Batch(1, 0))
                    mean1(Batch(1, 0))

            def emit(B, prev, prev2, nxt, prep):
                u, n = Turns(B, nxt, prev), 0
                for k in range(STEPS):
                    for c in range(NC):
                        if nxt:
                            maximum(B.plus(1), u, n, k, c)
                            n += 1
                        at = k, c
                        if prev2:
                            before = B.plus(-2)
                            if at == (0, 0):
                                mask_places(before)
                            if at == (0, 1):
                                sum_places(before)
                            if at == (0, 2):
                                number_tokens(before)
                            if at == (0, 3):
                                next_tokens(before)
                                invert_gate(before)
                            if at == (1, 0):
                                store_gate(before)
                        if prev:
                            before = B.plus(-1)
                            if at == (1, 0):
                                turn_sums(before, 1)
                            if at == (1, 2):
                                invert_sums(before, 1)
                            if at == (1, 3):
                                spread_sums(1)
                            if at == (2, 0):
                                turn_back(before)
                            if at == (3, 3):
                                stats2(before)
                            if at == (4, 0):
                                mean2(before)
                            if at == (6, 3):
                                take_logits(before, u, n)
                                n += 1
                            if at == (7, 0):
                                find_top(before, u, n - 2 if nxt else n - 1)
                            if at == (7, 1):
                                find_expert(before)
                            if at == (7, 2):
                                expert_number(before)
                            if at == (7, 3):
                                mark_expert(before)
                        if prep and at == (2, 1):
                            stats1(B.plus(3))
                        if prep and at == (2, 3):
                            mean1(B.plus(3))
                        if at == (5, 3) and prev:
                            n += 1
                        if at == (6, 0):
                            turn_sums(B, 0)
                        if at == (6, 1):
                            invert_sums(B, 0)
                        if at == (6, 2):
                            spread_sums(0)
                    if k % NC == NC - 1 and nxt:
                        split_maxima(B.plus(1), u, n, k // NC)
                        n += 1
                if prev:
                    take_ranks(B.plus(-1), u, n)

            rounds(dve, emit, lambda: (chain, chain.n, DVE_BATCH))
            last, u = Batch(7, 1), end_turns
            turn_sums(last, 1)
            invert_sums(last, 1)
            spread_sums(1)
            turn_back(last)

            def finish(B):
                mask_places(B)
                sum_places(B)
                number_tokens(B)
                next_tokens(B)
                invert_gate(B)
                store_gate(B)

            finish(last.plus(-1))
            stats2(last)
            mean2(last)
            take_logits(last, u, 1)
            find_top(last, u, 1)
            find_expert(last)
            expert_number(last)
            mark_expert(last)
            take_ranks(last, u, 2)
            finish(last)

            dve.wait_ge(ring_free, u.reads(3))
            for step in (
                lambda: nc.vector.scalar_tensor_tensor(counts_n[:], expert_iota[:], -float(CAP), count[:], ALU.mult, ALU.add),
                lambda: nc.vector.tensor_tensor(fill[:], counts_n[:].unsqueeze(2).to_broadcast([128, NE, NB]),
                                                block_iota[:], ALU.is_gt),
                lambda: nc.vector.reduce_sum(tiles[:], fill[:], AX.X),
                lambda: nc.vector.tensor_tensor(tri[:], up_to[:], tiles[:].unsqueeze(1).to_broadcast([128, NE, NE]),
                                                ALU.mult),
                lambda: nc.vector.reduce_sum(ends[:], tri[:], AX.X),
                lambda: nc.vector.tensor_scalar(passed[:], ends[:], slot_iota[:], None, ALU.is_le),
                lambda: nc.vector.reduce_sum(slot_f[:, 0:1], passed[:], AX.X),
                lambda: nc.vector.tensor_tensor(passed[:], passed[:], tiles[:], ALU.mult),
                lambda: nc.vector.reduce_sum(slot_f[:, 1:2], passed[:], AX.X),
                lambda: nc.vector.scalar_tensor_tensor(slot_f[:, 2:3], slot_f[:, 0:1], float(CAP // 128), slot_iota[:],
                                                       ALU.mult, ALU.add),
                lambda: nc.vector.tensor_tensor(slot_f[:, 2:3], slot_f[:, 2:3], slot_f[:, 1:2], ALU.subtract),
                lambda: nc.vector.tensor_scalar(slot_f[:, 3:4], slot_f[:, 0:1], float(NE - 1), None, ALU.min),
            ):
                chain.add(step())
                chain.settle()
            nc.vector.tensor_copy(slot_block[:], slot_f[:, 2:3]).then_inc(slots_ready, 1)
            dve.wait_ge(ring_full, u.fulls(4))
            nc.vector.tensor_copy(slot_expert[:], ps_ring[0:1, u.slot(3), 0:128]).then_inc(expert_ready, 1)
            dve.wait_ge(tokens_in, 16)
            nc.vector.tensor_copy(slot_tokens_f[:], slot_tokens[:]).then_inc(tokens_f, 1)
            dve.wait_ge(ring_full, u.fulls(5))
            nc.vector.tensor_copy(token_cols[:], ps_ring[:, u.slot(4), 0:32]).then_inc(cols_ready, 1)
            dve.wait_ge(bias_in, 16)
            dve.wait_ge(expert_ready, 1)

            def combine(s, i, r):
                e = nc.vector.value_load(slot_expert[0:1, bass.ds(s, 1)],
                                         min_val=0, max_val=NE - 1)
                dve.wait_ge(y_full, s + 1)
                nc.vector.tensor_tensor(y_sum[r % 2], ps_y[:, r % 2],
                                        bias_sb[:, bass.ds(e, 1)].rearrange("p o n -> p (o n)"), ALU.add).then_inc(y_read, 1)
                dve.wait_ge(y_read, s + 1)
                wait(dve, y_stored[r], i * 16)
                nc.vector.scalar_tensor_tensor(y_out[r], y_sum[r % 2], recs_in[r][:, 2 * DM:2 * DM + 1],
                                               recs_in[r][:, DM:2 * DM], ALU.mult, ALU.add).then_inc(y_ready, 1)

            for r in range(NREC):
                combine(r, 0, r)
            with dve.Fori(1, NSLOT // NREC) as i:
                for r in range(NREC):
                    combine(i * NREC + r, i, r)
            for s in range(NSLOT // NREC * NREC, NSLOT):
                combine(s, s // NREC, s % NREC)

        @block.tensor
        def _(pe):
            def turn_free(B, u, n):
                if u.rows_at is not None and u.rows_at == n - 2:
                    pe.wait_ge(rows_taken, B.b)
                else:
                    wait(pe, ring_free, u.reads(n - 1))

            def scores_for_max(B, u, n, k, chunks=range(NC)):
                g, j = divmod(k, NJ)
                if j == 0 and 0 in chunks:
                    pe.wait_ge(stack_in[B.p][g], B.i * (16 * 10) + 16 * 10)
                for c in chunks:
                    turn_free(B.plus(-1), u, n + c)
                    nc.tensor.matmul(ps_ring[:, u.slot(n + c)], q_stack[0:KA, B.p, g, j, c * 128:(c + 1) * 128],
                                     k_stack[0:KA, B.p, g, j], start=True, stop=True).then_inc(ring_full, 1)

            def turn_maxima(B, u, n, g):
                pe.wait_ge(ring_free, u.reads(n))
                nc.tensor.transpose(ps_ring[0:NJ * NC, u.slot(n), 0:128], neg_max[:, g].rearrange("p j c -> p (j c)"),
                                    identity[:]).then_inc(ring_full, 1)

            def scores(B, k, jp):
                g, c = divmod(k, NC)
                if c == 0 and jp == 0:
                    pe.wait_ge(shift_in[g], B.b * 48 + 48)
                wait(pe, exp_done, B.b * (2 * STEPS) + (2 * k + jp - 1))
                for j in (2 * jp, 2 * jp + 1):
                    last = nc.tensor.matmul(ps_scores[:, jp, j % 2], k_stack[0:KA, B.p, g, j, c * 128:(c + 1) * 128],
                                            q_stack[0:KA, B.p, g, j], start=True, stop=True)
                last.then_inc(scores_ready, 1)

            def values(B, k):
                g, c = divmod(k, NC)
                pe.wait_ge(exp_done, B.b * (2 * STEPS) + (2 * k + 2))
                if k == 0:
                    pe.wait_ge(v_ready, B.b + 1)
                if c == 0:
                    wait(pe, (low_turned, high_read)[g], B.b)
                for j in range(NJ):
                    last = nc.tensor.matmul(ps_pv[32 * j:32 * j + 32, g], v_ones[:, B.p, c, g, j], probs[:, k % 2, j],
                                            start=c == 0, stop=c == NC - 1)
                last.then_inc(pv_done, 1)

            def turn_rows(B, u, n):
                pe.wait_ge(xn2_ready, B.b + 1)
                turn_free(B.plus(1), u, n)
                for c in range(NC):
                    last = nc.tensor.transpose(ps_ring[:, u.slot(n), c * 128:(c + 1) * 128], rec[:, c * 128:(c + 1) * 128],
                                               identity[:])
                last.then_inc(ring_full, 1)

            def route(B, u, n):
                turn_free(B.plus(1), u, n)
                pe.wait_ge(rows_taken, B.b + 1)
                for c in range(NC):
                    last = nc.tensor.matmul(ps_ring[:, u.slot(n), 0:NE], xt[:, 0, c], wg_sb[:, c], start=c == 0,
                                            stop=c == NC - 1)
                last.then_inc(ring_full, 1)

            def rank(B, u, n):
                pe.wait_ge(onehot_ready, B.b + 1)
                turn_free(B.plus(1), u, n)
                for m, left in enumerate((earlier, ones_bf)):
                    last = nc.tensor.matmul(ps_ring[:, u.slot(n), m * NE:(m + 1) * NE], left[:], onehot[:], start=True,
                                            stop=True)
                last.then_inc(ring_full, 1)

            pe.wait_ge(pool_const, POOL_CONSTS)
            pe.wait_ge(dve_const, DVE_CONSTS)
            pe.wait_ge(consts_in, 16 * 3)
            n = 0
            for k in range(STEPS):
                scores_for_max(Batch(0, 0), start_turns, n, k)
                n += NC
                if k % NC == NC - 1:
                    turn_maxima(Batch(0, 0), start_turns, n, k // NC)
                    n += 1

            def emit(B, prev, prev2, nxt, prep):
                u, n = Turns(B, nxt, prev), 0
                for k in range(STEPS):
                    scores(B, k, 0)
                    if nxt:
                        scores_for_max(B.plus(1), u, n, k, (0,))
                    scores(B, k, 1)
                    if nxt:
                        scores_for_max(B.plus(1), u, n, k, (1, 2))
                    if k > 0:
                        values(B, k - 1)
                    elif prev:
                        values(B.plus(-1), STEPS - 1)
                    if nxt:
                        scores_for_max(B.plus(1), u, n, k, (3,))
                        n += NC
                    if k == 3 and nxt:
                        turn_maxima(B.plus(1), u, n, 0)
                        n += 1
                    if k == 5 and prev:
                        turn_rows(B.plus(-1), u, n)
                        n += 1
                    if k == 6 and prev:
                        route(B.plus(-1), u, n)
                        n += 1
                    if k == 7 and nxt:
                        turn_maxima(B.plus(1), u, n, 1)
                        n += 1
                    if k == 7 and prev:
                        rank(B.plus(-1), u, n)

            rounds(pe, emit)
            last, u = Batch(7, 1), end_turns
            values(last, STEPS - 1)
            turn_rows(last, u, 0)
            route(last, u, 1)
            rank(last, u, 2)
            pe.wait_ge(slots_ready, 1)
            pe.wait_ge(ring_free, u.reads(3))
            nc.tensor.transpose(ps_ring[0:1, u.slot(3), 0:128], slot_f[:, 3:4], identity[:]).then_inc(ring_full, 1)
            pe.wait_ge(tokens_f, 1)
            nc.tensor.transpose(ps_ring[:, u.slot(4), 0:32], slot_tokens_f[:], identity[0:32, 0:32]).then_inc(ring_full, 1)
            pe.wait_ge(expert_ready, 1)
            pe.wait_ge(w_loaded, 16 * NB)

            def turn_slot(s, i, r):
                pe.wait_ge(rec_in[r], i * 16 + 16)
                wait(pe, f_xt_ready, s - 1)
                for c in range(NC):
                    last = nc.tensor.transpose(ps_xt[:, r % 2, c * 128:(c + 1) * 128], recs_in[r][:, c * 128:(c + 1) * 128],
                                               identity[:])
                last.then_inc(f_xt_full, 1)

            def expert(s, r):
                e = nc.tensor.value_load(slot_expert[0:1, bass.ds(s, 1)],
                                         min_val=0, max_val=NE - 1)
                pe.wait_ge(f_xt_ready, s + 1)
                wait(pe, y_read, s - 1)
                for c in range(NC):
                    last = nc.tensor.matmul(ps_y[:, r % 2], xt[:, r % 2, c],
                                            w_sb[:, c, bass.ds(e, 1)].rearrange("p o n -> p (o n)"),
                                            start=c == 0, stop=c == NC - 1)
                last.then_inc(y_full, 1)

            turn_slot(0, 0, 0)
            for r in range(NREC):
                turn_slot(r + 1, (r + 1) // NREC, (r + 1) % NREC)
                expert(r, r)
            with pe.Fori(1, (NSLOT - 1) // NREC) as i:
                for r in range(NREC):
                    turn_slot(i * NREC + (r + 1), i + (r + 1) // NREC, (r + 1) % NREC)
                    expert(i * NREC + r, r)
            for s in range((NSLOT - 1) // NREC * NREC, NSLOT):
                if s + 1 < NSLOT:
                    turn_slot(s + 1, (s + 1) // NREC, (s + 1) % NREC)
                expert(s, s % NREC)


def kernel(x, ctx_2048, g_xattn, g_ffn, L0_ffn_wg, L0_ffn_W, L0_ffn_b):
    import numpy as np
    import concourse.bacc as bacc
    from concourse import mybir as mb
    from concourse.bass_utils import run_bass_kernel_spmd as run

    x = np.ascontiguousarray(x)
    c = np.ascontiguousarray(ctx_2048)

    def feature_first(a):
        return a.reshape(NB, NJ, NG, DH, DM).transpose(0, 3, 2, 1, 4).reshape(NB, ROWS, DM)

    arrays = {
        "x_rows": x,
        "x_perm": feature_first(x),
        "k_perm": feature_first(c),
        "v_t": c.reshape(NB, NJ, NG, DH, NC, 128).transpose(0, 5, 4, 2, 1, 3).reshape(NB, 128, DM),
        "w_t": np.asarray(L0_ffn_W).transpose(2, 0, 1).reshape(NC, 128, NE * DM).transpose(1, 0, 2)
               .reshape(128, NB, NC * NE * DM // NB).transpose(1, 0, 2),
        "wg_t": np.asarray(L0_ffn_wg).reshape(NC, 128, NE).transpose(1, 0, 2).reshape(128, NC * NE),
        "bias": np.asarray(L0_ffn_b).reshape(NE * DM),
        "g_attn": np.asarray(g_xattn).reshape(1),
        "g_ffn": np.asarray(g_ffn).reshape(1),
    }
    arrays = {name: np.ascontiguousarray(a) for name, a in arrays.items()}
    nc = bacc.Bacc("TRN2", target_bir_lowering=False, num_devices=1)
    args = {name: nc.dram_tensor(name, a.shape, mb.dt.from_np(a.dtype), kind="ExternalInput").ap()
            for name, a in arrays.items()}
    out = nc.dram_tensor("out", [NT, DM], F32, kind="ExternalOutput").ap()
    build(nc, out=out, **args)
    r = run(nc, [arrays], core_ids=[0])
    return r.results[0]["out"].reshape(NB, ROWS, DM)
```

```python
import concourse.bass as bass
from concourse import mybir
from contextlib import ExitStack

F32, BF16, I32, U32 = mybir.dt.float32, mybir.dt.bfloat16, mybir.dt.int32, mybir.dt.uint32
ALU = mybir.AluOpType
ACT = mybir.ActivationFunctionType
AX = mybir.AxisListType

NB, ROWS, DM = 16, 128, 512
NH, DH = 8, 16
NG, NJ = 2, 4
NC = DM // 128
STEPS = NG * NC
NP = 3
TERMS = 6
KS = TERMS * DH
KA = 128
EPS = 1e-5
NE = 8
NT = NB * ROWS
CAP = NT
NSLOT = NT // 128 + NE - 1
EARLY = -(-((NB - 2) * ROWS - 127 * NE) // 128)
NONE = 2 * NT
REC = 2 * DM + 4
NREC = 4
RING_FIRST, RING_BATCH = 33, 34
DVE_BATCH, POOL_BATCH = 8, 18


class Batch:

    def __init__(self, i, p):
        self.i, self.p = i + p // 2, p % 2
        self.b = self.i * 2 + self.p

    def known(self, b):
        return isinstance(self.b, int) and self.b == b

    def plus(self, n):
        return Batch(self.i, self.p + n) if n >= 0 else Batch(self.i - 1, self.p + n + 2)


class Chain:

    def __init__(self, eng, sem):
        self.eng, self.sem, self.base, self.n = eng, sem, 0, 0

    def add(self, op):
        op.then_inc(self.sem, 1)
        self.n += 1

    def settle(self):
        self.eng.wait_ge(self.sem, self.base + self.n)


def wait(eng, sem, value):
    if not isinstance(value, int) or value > 0:
        eng.wait_ge(sem, value)


def stand_alone(eng):
    eng.nop(nofuse=True)


class Turns:

    def __init__(self, base):
        self.base = base
        self.odd = base if isinstance(base, int) else RING_FIRST

    def at(self, n):
        return self.base + n

    def slot(self, n):
        return (self.odd + n) % 2

    def free(self, n):
        return self.base + (n - 1)


def ring_of(B):
    return Turns(B.b * RING_BATCH + RING_FIRST)


def build(nc, x_rows, x_perm, k_perm, v_t, w_t, wg_t, bias, g_attn, g_ffn, out):
    ctx = ExitStack()
    with ctx:
        def sb(name, shape, dt=F32):
            return ctx.enter_context(nc.sbuf_tensor(name, shape, dt))

        def sem(name):
            return ctx.enter_context(nc.semaphore(name))

        parts_dram = nc.dram_tensor("parts_dram", [NB, 2, NP, ROWS, DM], BF16, kind="Internal").ap()
        recs_dram = nc.dram_tensor("recs_dram", [NT, REC], F32, kind="Internal").ap()
        table_dram = nc.dram_tensor("table_dram", [NE * CAP, 1], I32, kind="Internal").ap()
        table_blocks = table_dram.rearrange("(k p) o -> k (p o)", p=128)

        identity = sb("identity", [128, 128])
        earlier = sb("earlier", [128, 128], BF16)
        ones_bf = sb("ones_bf", [128, 128], BF16)
        low_half = sb("low_half", [128, 1])
        high_half = sb("high_half", [128, 1])
        gates = sb("gates", [128, 4])
        low_gate = sb("low_gate", [128, 1])
        high_gate = sb("high_gate", [128, 1])
        power = sb("power", [128, 1])
        minus = sb("minus", [128, 1])
        expert_iota = sb("expert_iota", [128, NE])
        block_iota = sb("block_iota", [128, NE, NB])
        up_to = sb("up_to", [128, NE, NE])
        slot_iota = sb("slot_iota", [128, 1])
        zeros = sb("zeros", [NP, NJ * DM], BF16)
        none_i = sb("none_i", [128, 128], I32)
        wg_sb = sb("wg_sb", [128, NC, NE])
        w_sb = sb("w_sb", [128, NC, NE, DM])
        prep = sb("prep", [128, 5 * DM + 2 * NP * DM // 2])
        xp_in, k_in, qn = (prep[:, n * DM:(n + 1) * DM] for n in range(3))
        resid = prep[:, 3 * DM:5 * DM].rearrange("p (s m) -> p s m", s=2)
        parts = prep[:, 5 * DM:].bitcast(BF16).rearrange("p (s t m) -> p s t m", s=2, t=NP)
        v_in = sb("v_in", [128, NC, NG, NJ, DH])
        x_in = sb("x_in", [128, DM])
        stacks = sb("stacks", [128, 2, 2, NG, NJ, DM], BF16)
        q_stack, k_stack = stacks[:, :, 0], stacks[:, :, 1]
        v_ones = sb("v_ones", [128, 2, NC, NG, NJ, 2 * DH])
        neg_max = sb("neg_max", [128, NG, NJ, NC])
        shift = sb("shift", [NJ * NC, NG, 128])
        shift_rest = sb("shift_rest", [NJ * NC, NG, 128])
        shift_parts = sb("shift_parts", [NJ * NC, NG, NP, 128], BF16)
        probs = sb("probs", [128, 2, NJ, DM])
        low_num = sb("low_num", [128, DM])
        high_num = sb("high_num", [128, DM])
        num = sb("num", [128, DM])
        den = sb("den", [128, DM])
        den_turned = sb("den_turned", [128, NG, DM])
        recip = sb("recip", [128, NG, DM // 32])
        recip_turned = sb("recip_turned", [128, DM])
        rec = sb("rec", [128, 2, REC])
        xt = sb("xt", [128, NC, 128])
        st1 = sb("st1", [128, 6])
        mv1 = sb("mv1", [128, 2])
        rs1 = sb("rs1", [128, 3])
        st2 = sb("st2", [128, 6])
        mv2 = sb("mv2", [128, 2])
        rs2 = sb("rs2", [128, 3])
        logits = sb("logits", [128, NE])
        top = sb("top", [128, 8])
        top_at = sb("top_at", [128, 8], U32)
        top_f = sb("top_f", [128, 1])
        neg_top = sb("neg_top", [128, 1])
        gate_exp = sb("gate_exp", [128, NE])
        gate_sum = sb("gate_sum", [128, 1])
        gate_inv = sb("gate_inv", [128, 1])
        onehot = sb("onehot", [128, NE], BF16)
        place = sb("place", [128, NE])
        dest_f = sb("dest_f", [128, 1])
        dest_i = sb("dest_i", [128, 1], I32)
        token_f = sb("token_f", [128, 1])
        token_i = sb("token_i", [128, 1], I32)
        count = sb("count", [128, NE])
        stack_words = stacks[:].rearrange("p a s g j m -> p (a s g j m)").bitcast(F32)
        bias_sb = stack_words[:, 0:NE * DM].rearrange("p (e n) -> p e n", e=NE)
        y_out = [stack_words[:, (NE + r) * DM:(NE + r + 1) * DM] for r in range(NREC)]
        recs_in = [prep[:, r * REC:(r + 1) * REC] for r in range(3)]
        recs_in.append(sb("rec_buf", [128, REC])[:])
        y_sum = [v_ones[:].rearrange("p a c g j d -> p (a c g j d)")[:, r * DM:(r + 1) * DM] for r in range(2)]
        f_xt = probs[:].rearrange("p a j m -> p (a j m)")[:, 0:2 * DM].rearrange("p (r c n) -> p r c n", r=2, c=NC)
        counts_n = sb("counts_n", [128, NE])
        fill = sb("fill", [128, NE, NB])
        tiles = sb("tiles", [128, NE])
        tri = sb("tri", [128, NE, NE])
        ends = sb("ends", [128, NE])
        passed = sb("passed", [128, NE])
        taken = sb("taken", [128, NE + 1])
        skip = sb("skip", [128, NE])
        slot_f = sb("slot_f", [128, 3])
        slot_block = sb("slot_block", [128, 1], I32)
        slot_expert = sb("slot_expert", [1, NSLOT], I32)
        slot_tokens = sb("slot_tokens", [32, 128], I32)
        slot_tokens_f = sb("slot_tokens_f", [32, 128])
        token_cols = sb("token_cols", [128, NSLOT], I32)

        ps_scores = ctx.enter_context(nc.psum_tensor("ps_scores", [128, 2, 2, DM], F32))
        ps_ring = ctx.enter_context(nc.psum_tensor("ps_ring", [128, 2, DM], F32))
        ps_pv = ctx.enter_context(nc.psum_tensor("ps_pv", [128, NG, DM], F32))
        ps_y = ps_scores[:, 0]
        ps_xt = ps_scores[:, 1]

        consts_in = sem("consts_in")
        table_set = sem("table_set")
        xk_in = sem("xk_in")
        pads_in = sem("pads_in")
        v_loaded = sem("v_loaded")
        x_loaded = sem("x_loaded")
        w_loaded = sem("w_loaded")
        parts_out = sem("parts_out")
        stack_in = [[sem(f"stack_in{p}{g}") for g in range(NG)] for p in range(2)]
        shift_in = [sem(f"shift_in{g}") for g in range(NG)]
        rec_out = [sem(f"rec_out{p}") for p in range(2)]
        table_out = sem("table_out")
        pool_const = sem("pool_const")
        dve_const = sem("dve_const")
        gates_ready = sem("gates_ready")
        ln1_stats, ln1_rstd, qn_ready = sem("ln1_stats"), sem("ln1_rstd"), sem("qn_ready")
        high_cast, mid_cast = sem("high_cast"), sem("mid_cast")
        rest_ready, low_ready = sem("rest_ready"), sem("low_ready")
        v_ready = sem("v_ready")
        ring_full, ring_free = sem("ring_full"), sem("ring_free")
        rows_full, rows_taken = sem("rows_full"), sem("rows_taken")
        logits_full, logits_taken = sem("logits_full"), sem("logits_taken")
        ranks_full, ranks_taken = sem("ranks_full"), sem("ranks_taken")
        experts_full, tokens_full = sem("experts_full"), sem("tokens_full")
        shift_ready = sem("shift_ready")
        scores_ready, exp_done, pv_done = sem("scores_ready"), sem("exp_done"), sem("pv_done")
        low_read, high_read = sem("low_read"), sem("high_read")
        low_turned, high_turned = sem("low_turned"), sem("high_turned")
        inverted, spread = sem("inverted"), sem("spread")
        recip_ready, x1_done = sem("recip_ready"), sem("x1_done")
        ln2_stats, ln2_rstd, xn2_ready = sem("ln2_stats"), sem("ln2_rstd"), sem("xn2_ready")
        top_ready, gate_summed = sem("top_ready"), sem("gate_summed")
        onehot_ready, dest_ready, gate_ready = sem("onehot_ready"), sem("dest_ready"), sem("gate_ready")
        dve_chain, pool_chain = sem("dve_chain"), sem("pool_chain")
        bias_in = sem("bias_in")
        slots_ready, expert_ready = sem("slots_ready"), sem("expert_ready")
        tokens_in, tokens_f, cols_ready = sem("tokens_in"), sem("tokens_f"), sem("cols_ready")
        rec_in = [sem(f"rec_in{r}") for r in range(NREC)]
        f_xt_full, f_xt_ready = sem("f_xt_full"), sem("f_xt_ready")
        y_full, y_read, y_ready = sem("y_full"), sem("y_read"), sem("y_ready")
        y_stored = [sem(f"y_stored{r}") for r in range(NREC)]

        STACK_CONSTS, VALUE_CONSTS = 3, 4
        DVE_CONSTS = 17
        POOL_CONSTS = 13
        block = ctx.enter_context(nc.Block())

        start_turns = Turns(0)
        rows_bank, ranks_bank = ps_pv[:, 0], ps_pv[:, 1]

        def rounds(eng, emit, after_first=None):
            for n in range(2):
                emit(Batch(n // 2, n % 2), n > 0, False, True, True)
            start = after_first() if after_first else None
            with eng.Fori(1, 6) as i:
                for p in range(2):
                    B = Batch(i, p)
                    if start is not None:
                        start[0].base, start[0].n = (i - 1) * (2 * start[2]) + (start[1] + p * start[2]), 0
                    emit(B, True, True, True, True)
                    if start is not None:
                        assert start[0].n == start[2], (start[0].n, start[2])
            if start is not None:
                start[0].base, start[0].n = start[1] + 10 * start[2], 0
            for n in range(12, NB):
                emit(Batch(n // 2, n % 2), True, True, n + 1 < NB, n + 3 < NB)

        @block.sync
        def _(sp):
            def load_rows_keys(B):
                wait(sp, rest_ready, B.b * 2)
                if not isinstance(B.b, int):
                    stand_alone(sp)
                sp.dma_start(xp_in[:], x_perm[bass.ds(B.b, 1)].rearrange("o p m -> (o p) m")).then_inc(xk_in, 16)
                sp.dma_start(k_in[:], k_perm[bass.ds(B.b, 1)].rearrange("o p m -> (o p) m")).then_inc(xk_in, 16)

            def load_values(B):
                wait(sp, v_ready, B.b)
                if not isinstance(B.b, int):
                    stand_alone(sp)
                sp.dma_start(v_in[:].rearrange("p c g j d -> p (c g j d)"),
                             v_t[bass.ds(B.b, 1)].rearrange("o p m -> (o p) m")).then_inc(v_loaded, 16)

            def load_residual(B):
                wait(sp, x1_done, B.b)
                if not isinstance(B.b, int):
                    stand_alone(sp)
                sp.dma_start(x_in[:], x_rows[bass.ds(B.b, 1)].rearrange("o p m -> (o p) m")).then_inc(x_loaded, 16)

            def load_stack(B, g):
                wait(sp, parts_out, B.b * 16 + 16)
                if not isinstance(B.b, int):
                    stand_alone(sp)
                wait(sp, scores_ready, B.b * (2 * STEPS) + (STEPS * (g + 1) - 4 * STEPS))
                if not isinstance(B.b, int):
                    stand_alone(sp)
                mine = parts_dram[bass.ds(B.b, 1)].rearrange("o s t (c g j) m -> s (o g) t c (j m)", g=NG, j=NJ)
                for t, (first, n) in enumerate(((0, 3), (3, 2), (5, 1))):
                    sp.dma_start(q_stack[first * DH:(first + n) * DH, B.p, g].rearrange("p j m -> p (j m)"),
                                 mine[0, g, t].unsqueeze(0).to_broadcast([n, DH, NJ * DM])
                                 ).then_inc(stack_in[B.p][g], 16)
                for first, n in ((0, 3), (3, 2), (5, 1)):
                    sp.dma_start(k_stack[first * DH:(first + n) * DH, B.p, g].rearrange("p j m -> p (j m)"),
                                 mine[1, g, 0:n].rearrange("t c m -> (t c) m")).then_inc(stack_in[B.p][g], 16)
                if B.known(0) and g == 0:
                    sp.wait_ge(pads_in, 16)
                sp.dma_start(q_stack[KS:KS + NP, B.p, g].rearrange("p j m -> p (j m)"),
                             zeros[:]).then_inc(stack_in[B.p][g], 16)

            def load_shift(B, g):
                sp.wait_ge(shift_ready, B.b * 2 + (g + 1))
                for t in range(NP):
                    sp.dma_start(q_stack[KS + t:KS + t + 1, B.p, g].rearrange("o j (c m) -> o (j c) m", c=NC),
                                 shift_parts[:, g, t]).then_inc(shift_in[g], 16)

            def load_weights(B):
                n = NC * NE * DM // NB
                sp.dma_start(w_sb[:].rearrange("p c e n -> p (c e n)")[:, bass.ds(B.b * n, n)],
                             w_t[bass.ds(B.b, 1)].rearrange("o p n -> (o p) n")).then_inc(w_loaded, 16)

            def store_record(B):
                sp.wait_ge(gate_ready, B.b + 1)
                stand_alone(sp)
                sp.dma_start(recs_dram[bass.ds(B.b * ROWS, ROWS)], rec[:, B.p]).then_inc(rec_out[B.p], 16)

            load_rows_keys(Batch(0, 0))
            sp.dma_start(gates[:, 0:1], g_attn.partition_broadcast(128)).then_inc(consts_in, 16)
            sp.dma_start(gates[:, 1:2], g_ffn.partition_broadcast(128)).then_inc(consts_in, 16)
            sp.dma_start(wg_sb[:].rearrange("p c e -> p (c e)"), wg_t).then_inc(consts_in, 16)
            load_values(Batch(0, 0))
            load_rows_keys(Batch(0, 1))
            sp.wait_ge(dve_const, STACK_CONSTS)
            sp.dma_start(stacks[KS:KA, 1].rearrange("p s g j m -> p (s g j m)"),
                         stacks[KS:KA, 0].rearrange("p s g j m -> p (s g j m)")).then_inc(pads_in, 16)
            for g in range(NG):
                load_stack(Batch(0, 0), g)
            load_rows_keys(Batch(1, 0))
            for g in range(NG):
                load_stack(Batch(0, 1), g)
            load_shift(Batch(0, 0), 0)
            sp.wait_ge(pool_const, POOL_CONSTS)
            sp.dma_start(table_dram.rearrange("(k p) o -> k (p o)", p=128), none_i[:]).then_inc(table_set, 16)
            load_values(Batch(0, 1))
            load_rows_keys(Batch(1, 1))

            def emit(B, prev, prev2, nxt, prep):
                load_weights(B)
                load_shift(B, 1)
                if B.known(NB - 1):
                    sp.wait_ge(scores_ready, 2 * STEPS * (NB - 1))
                    sp.dma_start(bias_sb.rearrange("p e n -> p (e n)"), bias.partition_broadcast(128)).then_inc(bias_in, 16)
                if prev2:
                    store_record(B.plus(-2))
                stack = not isinstance(B.b, int) or B.b + 2 < NB
                load_residual(B)
                if stack:
                    load_stack(B.plus(2), 0)
                if not isinstance(B.b, int) or B.b + 4 < NB:
                    load_rows_keys(B.plus(4))
                if nxt:
                    load_shift(B.plus(1), 0)
                if stack:
                    load_stack(B.plus(2), 1)
                    load_values(B.plus(2))

            rounds(sp, emit)
            store_record(Batch(7, 0))
            store_record(Batch(7, 1))

        @block.gpsimd
        def _(pool):
            chain = Chain(pool, pool_chain)
            steps = [lambda: nc.gpsimd.memset(identity[:], 0.0),
                     lambda: nc.gpsimd.affine_select(out=identity[:], in_=identity[:], compare_op=ALU.not_equal, fill=1.0,
                                                     base=0, pattern=[[-1, 128]], channel_multiplier=1),
                     lambda: nc.gpsimd.memset(earlier[:], 1.0),
                     lambda: nc.gpsimd.affine_select(out=earlier[:], in_=earlier[:], compare_op=ALU.is_gt, fill=0.0,
                                                     base=0, pattern=[[1, 128]], channel_multiplier=-1),
                     lambda: nc.gpsimd.memset(ones_bf[:], 1.0),
                     lambda: nc.gpsimd.memset(power[:], -0.5),
                     lambda: nc.gpsimd.memset(minus[:], -1.0),
                     lambda: nc.gpsimd.iota(none_i[:], [[0, 128]], base=NONE, channel_multiplier=0),
                     lambda: nc.gpsimd.iota(expert_iota[:], [[1, NE]], base=0, channel_multiplier=0,
                                            allow_small_or_imprecise_dtypes=True),
                     lambda: nc.gpsimd.iota(block_iota[:], [[0, NE], [128, NB]], base=0, channel_multiplier=0,
                                            allow_small_or_imprecise_dtypes=True),
                     lambda: nc.gpsimd.iota(slot_iota[:], [[0, 1]], base=0, channel_multiplier=1,
                                            allow_small_or_imprecise_dtypes=True),
                     lambda: nc.gpsimd.iota(token_f[:], [[0, 1]], base=0, channel_multiplier=1,
                                            allow_small_or_imprecise_dtypes=True),
                     lambda: nc.gpsimd.iota(count[:], [[CAP, NE]], base=0, channel_multiplier=0,
                                            allow_small_or_imprecise_dtypes=True)]
            assert len(steps) == POOL_CONSTS
            for n, step in enumerate(steps):
                step().then_inc(pool_const, 1)
                pool.wait_ge(pool_const, n + 1)

            def rstd(B, stats, mv, rs, done, scale):
                pool.wait_ge(stats, B.b + 1)
                stand_alone(pool)
                chain.add(nc.gpsimd.tensor_scalar(rs[:, 0:1], mv[:, 1:2], EPS, scale, ALU.add, ALU.mult))
                chain.settle()
                chain.add(nc.gpsimd.tensor_tensor(rs[:, 1:2], rs[:, 0:1], power[:], ALU.pow))
                chain.settle()
                chain.add(nc.gpsimd.tensor_tensor(rs[:, 0:1], rs[:, 1:2], mv[:, 0:1], ALU.mult))
                chain.settle()
                nc.gpsimd.tensor_tensor(rs[:, 2:3], rs[:, 0:1], minus[:], ALU.mult).then_inc(done, 1)

            def rstd1(B):
                wait(pool, qn_ready, B.b)
                rstd(B, ln1_stats, mv1, rs1, ln1_rstd, float(DH))

            def rstd2(B):
                wait(pool, xn2_ready, B.b)
                rstd(B, ln2_stats, mv2, rs2, ln2_rstd, 1.0)

            def copy_values(B):
                pool.wait_ge(v_loaded, B.b * 16 + 16)
                wait(pool, pv_done, (B.b - 1) * STEPS)
                stand_alone(pool)
                chain.add(nc.gpsimd.tensor_copy(v_ones[:, B.p, :, 0, :, 0:DH], v_in[:, :, 0]))
                nc.gpsimd.tensor_copy(v_ones[:, B.p, :, 1, :, DH:2 * DH], v_in[:, :, 1]).then_inc(v_ready, 1)

            def rests(B):
                for n, (s, src) in enumerate(((1, k_in), (0, qn))):
                    pool.wait_ge(high_cast, B.b * 2 + (n + 1))
                    wait(pool, low_ready, B.b * 2)
                    nc.gpsimd.tensor_tensor(resid[:, s], src[:], parts[:, s, 0], ALU.subtract).then_inc(rest_ready, 1)

            def lows(B):
                for n, s in enumerate((1, 0)):
                    pool.wait_ge(mid_cast, B.b * 2 + (n + 1))
                    nc.gpsimd.tensor_tensor(parts[:, s, 2], resid[:, s], parts[:, s, 1], ALU.subtract).then_inc(low_ready, 1)
                pool.wait_ge(low_ready, B.b * 2 + 2)
                pool.dma_start(parts_dram[bass.ds(B.b, 1)].rearrange("o s t p m -> p (o s t) m"),
                               parts[:].rearrange("p s t m -> p (s t) m")).then_inc(parts_out, 16)

            def add_attention(B):
                pool.wait_ge(high_read, B.b + 1)
                chain.add(nc.gpsimd.tensor_tensor(num[:], low_num[:], high_num[:], ALU.add))
                chain.settle()
                pool.wait_ge(recip_ready, B.b + 1)
                pool.wait_ge(x_loaded, B.b * 16 + 16)
                wait(pool, rec_out[B.p], B.i * 16)
                if not isinstance(B.b, int):
                    stand_alone(pool)
                chain.add(nc.gpsimd.tensor_tensor(num[:], num[:], den[:], ALU.mult))
                chain.settle()
                nc.gpsimd.tensor_tensor(rec[:, B.p, DM:2 * DM], num[:], x_in[:], ALU.add).then_inc(x1_done, 1)

            def split_maxima(B, g):
                if g == 1:
                    pool.wait_ge(ring_free, ring_of(B).at(1 if B.known(NB - 1) else 2))
                else:
                    pool.wait_ge(ring_free, start_turns.at(18) if B.known(0) else ring_of(B.plus(-1)).at(19))
                stand_alone(pool)
                chain.add(nc.gpsimd.tensor_copy(shift_parts[:, g, 0], shift[:, g]))
                chain.settle()
                chain.add(nc.gpsimd.tensor_tensor(shift_rest[:, g], shift[:, g], shift_parts[:, g, 0], ALU.subtract))
                chain.settle()
                if not isinstance(B.b, int):
                    stand_alone(pool)
                chain.add(nc.gpsimd.tensor_copy(shift_parts[:, g, 1], shift_rest[:, g]))
                chain.settle()
                nc.gpsimd.tensor_tensor(shift_parts[:, g, 2], shift_rest[:, g], shift_parts[:, g, 1],
                                        ALU.subtract).then_inc(shift_ready, 1)

            def store_tokens(B):
                pool.wait_ge(dest_ready, B.b + 1)
                if not isinstance(B.b, int):
                    stand_alone(pool)
                wait(pool, table_out, B.b * 16)
                if not isinstance(B.b, int):
                    stand_alone(pool)
                chain.settle()
                if not isinstance(B.b, int):
                    stand_alone(pool)
                chain.add(nc.gpsimd.tensor_copy(dest_i[:], dest_f[:]))
                chain.add(nc.gpsimd.tensor_copy(token_i[:], token_f[:]))
                chain.settle()
                stand_alone(pool)
                if B.known(0):
                    pool.wait_ge(table_set, 16)
                pool.indirect_dma_start(table_dram, bass.IndirectOffsetOnAxis(ap=dest_i[:, 0:1], axis=0),
                                        token_i[:], None).then_inc(table_out, 16)
                chain.add(nc.gpsimd.tensor_scalar(token_f[:], token_f[:], float(ROWS), None, ALU.add))

            def spread_sums(B, g):
                pool.wait_ge(inverted, B.b * 2 + (g + 1))
                if g == 0:
                    wait(pool, recip_ready, B.b)
                stand_alone(pool)
                to = 0 if g == 0 else DH
                nc.gpsimd.tensor_copy(recip_turned[:].rearrange("p (t c) -> p t c", c=32)[:, :, to:to + DH],
                                      recip[:, g].unsqueeze(2).to_broadcast([128, DM // 32, DH])).then_inc(spread, 1)

            def read_slots(first, slots, batches):
                pool.wait_ge(slots_ready, 1 if first == 0 else 2)
                pool.wait_ge(table_out, 16 * batches)
                pool.indirect_dma_start(slot_tokens[0:slots], None, table_blocks,
                                        bass.IndirectOffsetOnAxis(ap=slot_block[0:slots, 0:1], axis=0),
                                        bounds_check=NE * CAP // 128 - 1, oob_is_err=False).then_inc(tokens_in, 16)

            def gather(s, r):
                stored = (NB - 2 if s < EARLY else NB) * ROWS
                pool.indirect_dma_start(recs_in[r], None, recs_dram[0:stored],
                                        bass.IndirectOffsetOnAxis(ap=token_cols[:, s:s + 1], axis=0),
                                        bounds_check=stored - 1, oob_is_err=False).then_inc(rec_in[r], 16)

            def scatter(s, r):
                pool.wait_ge(y_ready, s + 1)
                pool.indirect_dma_start(out, bass.IndirectOffsetOnAxis(ap=token_cols[:, s:s + 1], axis=0),
                                        y_out[r], None,
                                        bounds_check=NT - 1, oob_is_err=False).then_inc(y_stored[r], 16)

            for n in range(3):
                B = Batch(n // 2, n % 2)
                rstd1(B)
                rests(B)
                lows(B)
                if n == 0:
                    pool.wait_ge(dve_const, VALUE_CONSTS)
                    copy_values(B)
            split_maxima(Batch(0, 0), 0)

            def emit(B, prev, prev2, nxt, prep):
                if prep:
                    rstd1(B.plus(3))
                split_maxima(B, 1)
                if prev:
                    spread_sums(B.plus(-1), 1)
                    if B.known(NB - 1):
                        store_tokens(B.plus(-2))
                    add_attention(B.plus(-1))
                if prep:
                    rests(B.plus(3))
                if prev:
                    rstd2(B.plus(-1))
                if prev2 and not B.known(NB - 1):
                    store_tokens(B.plus(-2))
                if B.known(NB - 1):
                    read_slots(0, EARLY, NB - 2)
                    pool.wait_ge(rec_out[1], 16 * (NB // 2 - 1))
                    pool.wait_ge(cols_ready, 1)
                    for r in range(NREC):
                        gather(r, r)
                if nxt:
                    split_maxima(B.plus(1), 0)
                if prep:
                    lows(B.plus(3))
                if nxt:
                    copy_values(B.plus(1))
                spread_sums(B, 0)

            rounds(pool, emit, lambda: (chain, chain.n, POOL_BATCH))
            last = Batch(7, 1)
            spread_sums(last, 1)
            rstd2(last)
            store_tokens(last.plus(-1))
            for s in range(NSLOT):
                if s == 2:
                    store_tokens(last)
                if s == 3:
                    read_slots(EARLY, NSLOT - EARLY, NB)
                scatter(s, s % NREC)
                if s + NREC == EARLY:
                    pool.wait_ge(cols_ready, 2)
                    for p in range(2):
                        pool.wait_ge(rec_out[p], 16 * NB // 2)
                if s + NREC < NSLOT:
                    gather(s + NREC, s % NREC)
            for r in range(NREC):
                pool.wait_ge(y_stored[r], 16 * len(range(r, NSLOT, NREC)))

        @block.scalar
        def _(act):
            act.wait_ge(consts_in, 16 * 3)
            nc.scalar.activation(gates[:, 2:4], gates[:, 0:2], ACT.Tanh).then_inc(gates_ready, 1)

            def norm1(B):
                act.wait_ge(ln1_rstd, B.b + 1)
                wait(act, rest_ready, B.b * 2)
                nc.scalar.activation(qn[:], xp_in[:], ACT.Identity, bias=rs1[:, 2:3], scale=rs1[:, 1:2]).then_inc(qn_ready, 1)

            def norm2(B):
                act.wait_ge(ln2_rstd, B.b + 1)
                nc.scalar.activation(rec[:, B.p, 0:DM], rec[:, B.p, DM:2 * DM], ACT.Identity, bias=rs2[:, 2:3],
                                     scale=rs2[:, 1:2]).then_inc(xn2_ready, 1)

            def take_rows(B):
                act.wait_ge(rows_full, B.b + 1)
                nc.scalar.copy(xt[:].rearrange("p c n -> p (c n)"), rows_bank).then_inc(rows_taken, 1)

            def cast_high(B, s):
                src, ready, value = ((qn, qn_ready, B.b + 1), (k_in, xk_in, B.b * 32 + 32))[s]
                act.wait_ge(ready, value)
                wait(act, parts_out, B.b * 16)
                nc.scalar.copy(parts[:, s, 0], src[:]).then_inc(high_cast, 1)

            def cast_mid(B):
                for n, s in enumerate((1, 0)):
                    act.wait_ge(rest_ready, B.b * 2 + (n + 1))
                    nc.scalar.copy(parts[:, s, 1], resid[:, s]).then_inc(mid_cast, 1)

            def read_low(B):
                act.wait_ge(pv_done, B.b * STEPS + NC)
                wait(act, x1_done, B.b)
                nc.scalar.mul(low_num[:], ps_pv[:, 0], low_gate[:]).then_inc(low_read, 1)

            def read_high(B):
                act.wait_ge(high_turned, B.b + 1)
                nc.scalar.mul(high_num[:], ps_pv[:, 1], high_gate[:]).then_inc(high_read, 1)

            def sum_gate(B):
                act.wait_ge(top_ready, B.b + 1)
                nc.scalar.activation(gate_exp[:], logits[:], ACT.Exp, bias=neg_top[:],
                                     accum_out=gate_sum[:]).then_inc(gate_summed, 1)

            def exps(B, k):
                for jp in range(2):
                    act.wait_ge(scores_ready, B.b * (2 * STEPS) + (2 * k + jp + 1))
                    if jp == 0:
                        wait(act, pv_done, B.b * STEPS + (k - 1))
                    nc.scalar.activation(probs[:, k % 2, 2 * jp:2 * jp + 2], ps_scores[:, jp], ACT.Exp).then_inc(exp_done, 1)

            for n in range(3):
                B = Batch(n // 2, n % 2)
                cast_high(B, 1)
                norm1(B)
                cast_high(B, 0)
                cast_mid(B)
            act.wait_ge(dve_const, DVE_CONSTS)

            def emit(B, prev, prev2, nxt, prep):
                for k in range(STEPS):
                    exps(B, k)
                    if k == 1 and prev:
                        read_high(B.plus(-1))
                    if k == 1 and prep:
                        norm1(B.plus(3))
                    if k == 2 and prev2:
                        sum_gate(B.plus(-2))
                    if k == 2 and prep:
                        cast_high(B.plus(3), 1)
                        cast_high(B.plus(3), 0)
                    if k == 3 and prep:
                        cast_mid(B.plus(3))
                    if k == (5 if B.known(NB - 1) else 4) and prev:
                        norm2(B.plus(-1))
                    if k == 5:
                        read_low(B)
                    if k == 7 and prev:
                        take_rows(B.plus(-1))

            rounds(act, emit)
            read_high(Batch(7, 1))

            def evacuate(s, r):
                act.wait_ge(f_xt_full, s + 1)
                wait(act, y_full, s - 1)
                nc.scalar.copy(f_xt[:, r % 2].rearrange("p c n -> p (c n)"), ps_xt[:, r % 2]).then_inc(f_xt_ready, 1)

            for s in range(5):
                if s == 2:
                    sum_gate(Batch(7, 0))
                if s == 3:
                    norm2(Batch(7, 1))
                    take_rows(Batch(7, 1))
                if s == 4:
                    sum_gate(Batch(7, 1))
                evacuate(s, s % 2)
            with act.Fori(2, (NSLOT - 1) // 2) as i:
                for r in range(2):
                    evacuate(i * 2 + (r + 1), r + 1)

        @block.vector
        def _(dve):
            chain = Chain(dve, dve_chain)
            first_steps = [lambda: nc.vector.memset(stacks[KS:KA, 0].rearrange("p s g j m -> p (s g j m)"), 0.0),
                           lambda: nc.vector.memset(stacks[KS:KS + NP, 0, 1].rearrange("p g j m -> p (g j m)"), 1.0),
                           lambda: nc.vector.memset(zeros[:], 0.0),
                           lambda: nc.vector.memset(v_ones[:].rearrange("p a c g j d -> p (a c g j d)"), 1.0)]
            steps = [lambda: nc.vector.memset(low_half[:], 0.0)]
            steps += [lambda j=j: nc.vector.memset(low_half[32 * j:32 * j + DH], 1.0) for j in range(NJ)]
            steps += [lambda: nc.vector.tensor_scalar(high_half[:], low_half[:], -1.0, 1.0, ALU.mult, ALU.add),
                      lambda: nc.vector.memset(rec[:, :, 2 * DM:REC], 0.0),
                      lambda: nc.vector.memset(recs_in[-1], 0.0),
                      lambda: nc.vector.memset(slot_tokens_f[:], float(NONE)),
                      lambda: nc.vector.tensor_copy(slot_tokens[:], slot_tokens_f[:]),
                      lambda: nc.vector.memset(up_to[:], 0.0)]
            steps += [lambda: nc.vector.tensor_scalar(low_gate[:], low_half[:], gates[:, 2:3], None, ALU.mult),
                      lambda: nc.vector.tensor_scalar(high_gate[:], high_half[:], gates[:, 2:3], None, ALU.mult)]
            assert len(first_steps) == VALUE_CONSTS and len(first_steps + steps) == DVE_CONSTS

            def set_constants(steps, first):
                for n, step in enumerate(steps):
                    step().then_inc(dve_const, 1)
                    dve.wait_ge(dve_const, first + n + 1)

            def maximum(u, n, k, c):
                g, j = divmod(k, NJ)
                dve.wait_ge(ring_full, u.at(n + 1))
                nc.vector.tensor_reduce(neg_max[:, g, j, c:c + 1], ps_ring[:, u.slot(n)], AX.X, ALU.max,
                                        negate=True).then_inc(ring_free, 1)

            def take_maxima(B, u, n, g):
                dve.wait_ge(ring_full, u.at(n + 1))
                wait(dve, shift_in[g], B.b * 48)
                nc.vector.tensor_copy(shift[:, g], ps_ring[0:NJ * NC, u.slot(n), 0:128]).then_inc(ring_free, 1)

            def stats1(B):
                dve.wait_ge(xk_in, B.b * 32 + 32)
                chain.add(nc.vector.bn_stats(st1[:], xp_in[:]))

            def mean1(B):
                chain.settle()
                stand_alone(dve)
                nc.vector.bn_aggr(mv1[:], st1[:]).then_inc(ln1_stats, 1)

            def turn_sums(B, g):
                if g == 0:
                    dve.wait_ge(low_read, B.b + 1)
                else:
                    dve.wait_ge(pv_done, B.b * STEPS + STEPS)
                nc.vector.transpose(den_turned[:, g], ps_pv[:, g]).then_inc((low_turned, high_turned)[g], 1)

            def invert_sums(B, g):
                dve.wait_ge((low_turned, high_turned)[g], B.b + 1)
                wait(dve, spread, B.b * 2 + (g - 1))
                at = DH if g == 0 else 0
                nc.vector.reciprocal(recip[:, g], den_turned[:, g].rearrange("p (t c) -> p t c", c=32)[:, :, at]
                                     ).then_inc(inverted, 1)

            def turn_back(B):
                dve.wait_ge(spread, B.b * 2 + 2)
                wait(dve, x1_done, B.b)
                nc.vector.transpose(den[:], recip_turned[:]).then_inc(recip_ready, 1)

            def stats2(B):
                dve.wait_ge(x1_done, B.b + 1)
                chain.add(nc.vector.bn_stats(st2[:], rec[:, B.p, DM:2 * DM]))

            def mean2(B):
                chain.settle()
                stand_alone(dve)
                nc.vector.bn_aggr(mv2[:], st2[:]).then_inc(ln2_stats, 1)

            def take_logits(B):
                dve.wait_ge(logits_full, B.b + 1)
                nc.vector.tensor_copy(logits[:], rows_bank[:, 0:NE]).then_inc(logits_taken, 1)

            def find_top(B):
                dve.wait_ge(logits_taken, B.b + 1)
                stand_alone(dve)
                chain.add(nc.vector.max(top[:], logits[:]))

            def find_expert(B):
                chain.settle()
                nc.vector.tensor_scalar(neg_top[:], top[:, 0:1], -1.0, None, ALU.mult).then_inc(top_ready, 1)
                chain.add(nc.vector.max_index(top_at[:], top[:], logits[:]))

            def expert_number(B):
                chain.settle()
                chain.add(nc.vector.tensor_copy(top_f[:], top_at[:, 0:1]))

            def mark_expert(B):
                chain.settle()
                nc.vector.tensor_scalar(onehot[:], expert_iota[:], top_f[:], None, ALU.is_equal).then_inc(onehot_ready, 1)

            def take_ranks(B, bank):
                dve.wait_ge(ranks_full, B.b + 1)
                chain.add(nc.vector.tensor_tensor(place[:], bank[:, 0:NE], count[:], ALU.add))
                chain.settle()
                nc.vector.tensor_tensor(count[:], count[:], bank[:, NE:2 * NE], ALU.add).then_inc(ranks_taken, 1)

            def mask_places(B):
                chain.settle()
                dve.wait_ge(onehot_ready, B.b + 1)
                chain.add(nc.vector.tensor_tensor(place[:], place[:], onehot[:], ALU.mult))

            def sum_places(B):
                chain.settle()
                wait(dve, table_out, B.b * 16)
                if not isinstance(B.b, int):
                    stand_alone(dve)
                nc.vector.reduce_sum(dest_f[:], place[:], AX.X).then_inc(dest_ready, 1)

            def invert_gate(B):
                dve.wait_ge(gate_summed, B.b + 1)
                chain.add(nc.vector.reciprocal(gate_inv[:], gate_sum[:]))

            def store_gate(B):
                chain.settle()
                nc.vector.tensor_scalar(rec[:, B.p, 2 * DM:2 * DM + 1], gate_inv[:], gates[:, 3:4], None,
                                        ALU.mult).then_inc(gate_ready, 1)

            def find_slots(early):
                dve.wait_ge(ranks_taken, NB - 2 if early else NB)
                steps = [
                    lambda: nc.vector.scalar_tensor_tensor(counts_n[:], expert_iota[:], -float(CAP), count[:], ALU.mult,
                                                           ALU.add)]
                if early:
                    steps += [lambda: nc.vector.tensor_scalar(counts_n[:], counts_n[:], -127.0, None, ALU.add)]
                steps += [
                    lambda: nc.vector.tensor_tensor(fill[:], counts_n[:].unsqueeze(2).to_broadcast([128, NE, NB]),
                                                    block_iota[:], ALU.is_gt),
                    lambda: nc.vector.reduce_sum(tiles[:], fill[:], AX.X)]
                if not early:
                    steps += [lambda: nc.vector.tensor_tensor(tiles[:], tiles[:], taken[:, 0:NE], ALU.subtract)]
                steps += [
                    lambda: nc.vector.tensor_tensor(tri[:], up_to[:],
                                                    tiles[:].unsqueeze(1).to_broadcast([128, NE, NE]), ALU.mult),
                    lambda: nc.vector.reduce_sum(ends[:], tri[:], AX.X),
                    lambda: nc.vector.tensor_scalar(passed[:], ends[:], slot_iota[:], None, ALU.is_le),
                    lambda: nc.vector.reduce_sum(slot_f[:, 0:1], passed[:], AX.X),
                    lambda: nc.vector.tensor_scalar(slot_f[:, 2:3], slot_f[:, 0:1], float(NE - 1), None, ALU.min),
                    lambda: nc.vector.tensor_tensor(skip[:], taken[:, 1:NE + 1], taken[:, 0:NE], ALU.subtract),
                    lambda: nc.vector.tensor_tensor(skip[:], skip[:], tiles[:], ALU.subtract),
                    lambda: nc.vector.tensor_scalar(skip[:], skip[:], float(CAP // 128), None, ALU.add),
                    lambda: nc.vector.tensor_tensor(skip[:], skip[:], passed[:], ALU.mult),
                    lambda: nc.vector.reduce_sum(slot_f[:, 1:2], skip[:], AX.X),
                    lambda: nc.vector.tensor_tensor(slot_f[:, 1:2], slot_f[:, 1:2], slot_iota[:], ALU.add),
                    lambda: nc.vector.tensor_tensor(slot_f[:, 1:2], slot_f[:, 1:2], taken[:, 0:1], ALU.add)]
                for step in steps:
                    chain.add(step())
                    chain.settle()
                nc.vector.tensor_copy(slot_block[:], slot_f[:, 1:2]).then_inc(slots_ready, 1)
                if early:
                    for step in (
                        lambda: nc.vector.tensor_tensor(skip[:], tiles[:], ends[:], ALU.subtract),
                        lambda: nc.vector.tensor_scalar(skip[:], skip[:], float(EARLY), 0.0, ALU.add, ALU.max),
                        lambda: nc.vector.tensor_tensor(taken[:, 0:NE], skip[:], tiles[:], ALU.min),
                    ):
                        chain.add(step())
                        chain.settle()

            def take_experts(first, slots, value):
                dve.wait_ge(experts_full, value)
                nc.vector.tensor_copy(slot_expert[0:1, first:first + slots],
                                      ps_ring[0:1, 0, 0:slots]).then_inc(expert_ready, 1)

            def tokens_to_float(value):
                dve.wait_ge(tokens_in, 16 * value)
                nc.vector.tensor_copy(slot_tokens_f[:], slot_tokens[:]).then_inc(tokens_f, 1)

            def take_columns(first, slots, value):
                dve.wait_ge(tokens_full, value)
                nc.vector.tensor_copy(token_cols[:, first:first + slots], ps_ring[:, 1, 0:slots]).then_inc(cols_ready, 1)

            def empty_slots():
                dve.wait_ge(cols_ready, 1)
                chain.add(nc.vector.memset(slot_tokens_f[:], float(NONE)))
                chain.settle()
                chain.add(nc.vector.tensor_copy(slot_tokens[:], slot_tokens_f[:]))

            def combine(s, i, r):
                e = nc.vector.value_load(slot_expert[0:1, bass.ds(s, 1)],
                                         min_val=0, max_val=NE - 1)
                dve.wait_ge(y_full, s + 1)
                nc.vector.tensor_tensor(y_sum[r % 2], ps_y[:, r % 2],
                                        bias_sb[:, bass.ds(e, 1)].rearrange("p o n -> p (o n)"), ALU.add).then_inc(y_read, 1)
                dve.wait_ge(y_read, s + 1)
                wait(dve, y_stored[r], i * 16)
                nc.vector.scalar_tensor_tensor(y_out[r], y_sum[r % 2], recs_in[r][:, 2 * DM:2 * DM + 1],
                                               recs_in[r][:, DM:2 * DM], ALU.mult, ALU.add).then_inc(y_ready, 1)

            stats1(Batch(0, 0))
            mean1(Batch(0, 0))
            set_constants(first_steps, 0)
            stats1(Batch(0, 1))
            mean1(Batch(0, 1))
            dve.wait_ge(gates_ready, 1)
            set_constants(steps, VALUE_CONSTS)
            for e in range(NE):
                chain.add(nc.vector.memset(up_to[:, e, 0:e + 1], 1.0))
            chain.add(nc.vector.memset(taken[:], 0.0))
            chain.settle()
            dve.wait_ge(pool_const, POOL_CONSTS)
            n = 0
            for k in range(STEPS):
                for c in range(NC):
                    maximum(start_turns, n, k, c)
                    n += 1
                    if (k, c) == (NC, 0):
                        take_maxima(Batch(0, 0), start_turns, n, 0)
                        n += 1
                if k == 2:
                    stats1(Batch(1, 0))
                    mean1(Batch(1, 0))

            def place_tokens(B, bank):
                take_ranks(B, bank)
                mask_places(B)
                sum_places(B)

            def emit(B, prev, prev2, nxt, prep):
                u, n = ring_of(B), 0
                for k in range(STEPS):
                    for c in range(NC):
                        at = k, c
                        if nxt:
                            maximum(u, n, k, c)
                            n += 1
                        if at == (0, 0):
                            take_maxima(B, u, n, 1)
                            n += 1
                        if at == (NC, 0) and nxt:
                            take_maxima(B.plus(1), u, n, 0)
                            n += 1
                        if prep and at == (0, 2):
                            stats1(B.plus(3))
                        if prep and at == (0, 3):
                            mean1(B.plus(3))
                        if prev2:
                            routed = B.plus(-2)
                            if at == (1, 0):
                                take_logits(routed)
                            if at == (1, 1):
                                find_top(routed)
                            if at == (1, 2):
                                find_expert(routed)
                            if at == (1, 3):
                                expert_number(routed)
                            if at == (2, 0):
                                mark_expert(routed)
                            if at == (2, 3):
                                invert_gate(routed)
                            if at == (3, 0):
                                store_gate(routed)
                            if B.known(NB - 1):
                                if at == (2, 0):
                                    place_tokens(routed, ps_ring[:, 0])
                                    find_slots(True)
                            else:
                                if at == (3, 0):
                                    take_ranks(routed, ranks_bank)
                                if at == (3, 1):
                                    mask_places(routed)
                                if at == (3, 2):
                                    sum_places(routed)
                        if prev:
                            attended = B.plus(-1)
                            if at == (0, 3):
                                turn_sums(attended, 1)
                            if at == (1, 0):
                                invert_sums(attended, 1)
                            if at == ((1, 3) if B.known(NB - 1) else (2, 1)):
                                turn_back(attended)
                            if at == (3, 2):
                                stats2(attended)
                            if at == (3, 3):
                                mean2(attended)
                        if at == (6, 2):
                            turn_sums(B, 0)
                        if B.known(NB - 1) and at == (6, 2):
                            tokens_to_float(1)
                        if at == (7, 1):
                            invert_sums(B, 0)
                        if B.known(NB - 1) and at == (7, 2):
                            take_experts(0, EARLY, 1)
                            take_columns(0, EARLY, 1)
                            empty_slots()

            rounds(dve, emit, lambda: (chain, chain.n, DVE_BATCH))

            def choose(B):
                take_logits(B)
                find_top(B)
                find_expert(B)
                expert_number(B)
                mark_expert(B)

            def add_attention(B):
                dve.wait_ge(high_read, B.b + 1)
                chain.add(nc.vector.tensor_tensor(num[:], low_num[:], high_num[:], ALU.add))
                chain.settle()
                dve.wait_ge(recip_ready, B.b + 1)
                dve.wait_ge(x_loaded, B.b * 16 + 16)
                dve.wait_ge(rec_out[B.p], B.i * 16)
                chain.add(nc.vector.tensor_tensor(num[:], num[:], den[:], ALU.mult))
                chain.settle()
                chain.add(nc.vector.tensor_tensor(rec[:, B.p, DM:2 * DM], num[:], x_in[:], ALU.add))
                chain.settle()
                chain.add(nc.vector.bn_stats(st2[:], rec[:, B.p, DM:2 * DM]))

            last = Batch(7, 1)
            turn_sums(last, 1)
            invert_sums(last, 1)
            turn_back(last)
            choose(last.plus(-1))
            add_attention(last)
            mean2(last)
            place_tokens(last.plus(-1), ps_ring[:, 0])
            invert_gate(last.plus(-1))
            store_gate(last.plus(-1))
            dve.wait_ge(bias_in, 16)
            dve.wait_ge(expert_ready, 1)
            combine(0, 0, 0)
            combine(1, 0, 1)
            choose(last)
            invert_gate(last)
            store_gate(last)
            place_tokens(last, ps_ring[:, 1])
            combine(2, 0, 2)
            find_slots(False)
            combine(3, 0, 3)
            tokens_to_float(2)
            take_experts(EARLY, NSLOT - EARLY, 2)
            take_columns(EARLY, NSLOT - EARLY, 2)
            combine(4, 1, 0)
            for s in range(5, 2 * NREC):
                combine(s, s // NREC, s % NREC)
            dve.wait_ge(expert_ready, 2)
            with dve.Fori(2, NSLOT // NREC) as i:
                for r in range(NREC):
                    combine(i * NREC + r, i, r)
            for s in range(NSLOT // NREC * NREC, NSLOT):
                combine(s, s // NREC, s % NREC)

        @block.tensor
        def _(pe):
            def scores_for_max(B, u, n, k, chunks=range(NC)):
                g, j = divmod(k, NJ)
                if j == 0 and 0 in chunks:
                    pe.wait_ge(stack_in[B.p][g], B.i * (16 * 7) + 16 * 7)
                for c in chunks:
                    wait(pe, ring_free, u.free(n + c))
                    nc.tensor.matmul(ps_ring[:, u.slot(n + c)], q_stack[0:KA, B.p, g, j, c * 128:(c + 1) * 128],
                                     k_stack[0:KA, B.p, g, j], start=True, stop=True).then_inc(ring_full, 1)

            def turn_maxima(B, u, n, g):
                pe.wait_ge(ring_free, u.free(max(n, 1)))
                nc.tensor.transpose(ps_ring[0:NJ * NC, u.slot(n), 0:128], neg_max[:, g].rearrange("p j c -> p (j c)"),
                                    identity[:]).then_inc(ring_full, 1)

            def scores(B, k, jp):
                g, c = divmod(k, NC)
                if c == 0 and jp == 0:
                    pe.wait_ge(shift_in[g], B.b * 48 + 48)
                wait(pe, exp_done, B.b * (2 * STEPS) + (2 * k + jp - 1))
                for j in (2 * jp, 2 * jp + 1):
                    last = nc.tensor.matmul(ps_scores[:, jp, j % 2], k_stack[0:KA, B.p, g, j, c * 128:(c + 1) * 128],
                                            q_stack[0:KA, B.p, g, j], start=True, stop=True)
                last.then_inc(scores_ready, 1)

            def values(B, k):
                g, c = divmod(k, NC)
                pe.wait_ge(exp_done, B.b * (2 * STEPS) + (2 * k + 2))
                if k == 0:
                    pe.wait_ge(v_ready, B.b + 1)
                if c == 0:
                    wait(pe, (low_turned, high_read)[g], B.b)
                    if not isinstance(B.b, int) or B.b > 1:
                        pe.wait_ge((logits_taken, ranks_taken)[g], B.b - 1)
                for j in range(NJ):
                    last = nc.tensor.matmul(ps_pv[32 * j:32 * j + 32, g], v_ones[:, B.p, c, g, j], probs[:, k % 2, j],
                                            start=c == 0, stop=c == NC - 1)
                last.then_inc(pv_done, 1)

            def turn_rows(B):
                pe.wait_ge(xn2_ready, B.b + 1)
                pe.wait_ge(low_turned, B.b + (1 if B.known(NB - 1) else 2))
                for c in range(NC):
                    last = nc.tensor.transpose(rows_bank[:, c * 128:(c + 1) * 128], rec[:, B.p, c * 128:(c + 1) * 128],
                                               identity[:])
                last.then_inc(rows_full, 1)

            def route(B):
                pe.wait_ge(rows_taken, B.b + 1)
                for c in range(NC):
                    last = nc.tensor.matmul(rows_bank[:, 0:NE], xt[:, c], wg_sb[:, c], start=c == 0, stop=c == NC - 1)
                last.then_inc(logits_full, 1)

            def rank(B, bank):
                pe.wait_ge(onehot_ready, B.b + 1)
                for m, left in enumerate((earlier, ones_bf)):
                    last = nc.tensor.matmul(bank[:, m * NE:(m + 1) * NE], left[:], onehot[:], start=True, stop=True)
                last.then_inc(ranks_full, 1)

            def turn_experts(value):
                pe.wait_ge(slots_ready, value)
                nc.tensor.transpose(ps_ring[0:1, 0, 0:128], slot_f[:, 2:3], identity[:]).then_inc(experts_full, 1)

            def turn_tokens(value):
                pe.wait_ge(tokens_f, value)
                nc.tensor.transpose(ps_ring[:, 1, 0:32], slot_tokens_f[:], identity[0:32, 0:32]).then_inc(tokens_full, 1)

            pe.wait_ge(pool_const, POOL_CONSTS)
            pe.wait_ge(dve_const, STACK_CONSTS)
            pe.wait_ge(consts_in, 16 * 3)
            n = 0
            for k in range(STEPS):
                for c in range(NC):
                    scores_for_max(Batch(0, 0), start_turns, n - c, k, (c,))
                    n += 1
                    if (k, c) == (NC, 0):
                        turn_maxima(Batch(0, 0), start_turns, n, 0)
                        n += 1

            def emit(B, prev, prev2, nxt, prep):
                u, n = ring_of(B), 0
                for k in range(STEPS):
                    scores(B, k, 0)
                    if nxt:
                        scores_for_max(B.plus(1), u, n, k, (0,))
                        n += 1
                    if k == 0:
                        turn_maxima(B, u, n, 1)
                        n += 1
                    if k == NC and nxt:
                        turn_maxima(B.plus(1), u, n, 0)
                        n += 1
                    scores(B, k, 1)
                    if nxt:
                        scores_for_max(B.plus(1), u, n - 1, k, (1, 2))
                        n += 2
                    if k > 0:
                        values(B, k - 1)
                    elif prev:
                        values(B.plus(-1), STEPS - 1)
                    if k == 1 and B.known(NB - 1):
                        rank(B.plus(-2), ps_ring[:, 0])
                    if k == 2 and prev2 and not B.known(NB - 1):
                        pe.wait_ge(high_read, B.b)
                        rank(B.plus(-2), ranks_bank)
                    if k == 7 and prev:
                        turn_rows(B.plus(-1))
                    if k == 6 and B.known(NB - 1):
                        turn_experts(1)
                        turn_tokens(1)
                    if nxt:
                        scores_for_max(B.plus(1), u, n - 3, k, (3,))
                        n += 1
                    if k == 0 and prev2:
                        route(B.plus(-2))

            pe.wait_ge(dve_const, DVE_CONSTS)
            rounds(pe, emit)

            def turn_slot(s, i, r):
                pe.wait_ge(rec_in[r], i * 16 + 16)
                wait(pe, f_xt_ready, s - 1)
                for c in range(NC):
                    last = nc.tensor.transpose(ps_xt[:, r % 2, c * 128:(c + 1) * 128], recs_in[r][:, c * 128:(c + 1) * 128],
                                               identity[:])
                last.then_inc(f_xt_full, 1)

            def expert(s, r, halfway=None):
                e = nc.tensor.value_load(slot_expert[0:1, bass.ds(s, 1)],
                                         min_val=0, max_val=NE - 1)
                pe.wait_ge(f_xt_ready, s + 1)
                wait(pe, y_read, s - 1)
                for c in range(NC):
                    if c == NC // 2 and halfway:
                        halfway()
                    last = nc.tensor.matmul(ps_y[:, r % 2], f_xt[:, r % 2, c],
                                            w_sb[:, c, bass.ds(e, 1)].rearrange("p o n -> p (o n)"),
                                            start=c == 0, stop=c == NC - 1)
                last.then_inc(y_full, 1)

            last = Batch(7, 1)
            route(last.plus(-1))
            values(last, STEPS - 1)
            pe.wait_ge(expert_ready, 1)
            pe.wait_ge(w_loaded, 16 * NB)
            def rank_last():
                pe.wait_ge(cols_ready, 1)
                rank(last, ps_ring[:, 1])

            turn_slot(0, 0, 0)
            for s in range(2 * NREC - 1):
                if s == 2:
                    turn_rows(last)
                turn_slot(s + 1, (s + 1) // NREC, (s + 1) % NREC)
                if s == 2:
                    route(last)
                if s == EARLY - 1:
                    pe.wait_ge(expert_ready, 2)
                expert(s, s % NREC, rank_last if s == 2 else None)
                if s == 0:
                    rank(last.plus(-1), ps_ring[:, 0])
                if s == 4:
                    pe.wait_ge(ranks_taken, NB)
                    turn_experts(2)
                    turn_tokens(2)
            turn_slot(2 * NREC, 2, 0)
            expert(2 * NREC - 1, NREC - 1)
            with pe.Fori(2, (NSLOT - 1) // NREC) as i:
                for r in range(NREC):
                    turn_slot(i * NREC + (r + 1), i + (r + 1) // NREC, (r + 1) % NREC)
                    expert(i * NREC + r, r)
            for s in range((NSLOT - 1) // NREC * NREC, NSLOT):
                if s + 1 < NSLOT:
                    turn_slot(s + 1, (s + 1) // NREC, (s + 1) % NREC)
                expert(s, s % NREC)


def kernel(x, ctx_2048, g_xattn, g_ffn, L0_ffn_wg, L0_ffn_W, L0_ffn_b):
    import numpy as np
    import concourse.bacc as bacc
    from concourse import mybir as mb
    from concourse.bass_utils import run_bass_kernel_spmd as run

    x = np.ascontiguousarray(x)
    c = np.ascontiguousarray(ctx_2048)

    def feature_first(a):
        return a.reshape(NB, NJ, NG, DH, DM).transpose(0, 3, 2, 1, 4).reshape(NB, ROWS, DM)

    arrays = {
        "x_rows": x,
        "x_perm": feature_first(x),
        "k_perm": feature_first(c),
        "v_t": c.reshape(NB, NJ, NG, DH, NC, 128).transpose(0, 5, 4, 2, 1, 3).reshape(NB, 128, DM),
        "w_t": np.asarray(L0_ffn_W).transpose(2, 0, 1).reshape(NC, 128, NE * DM).transpose(1, 0, 2)
               .reshape(128, NB, NC * NE * DM // NB).transpose(1, 0, 2),
        "wg_t": np.asarray(L0_ffn_wg).reshape(NC, 128, NE).transpose(1, 0, 2).reshape(128, NC * NE),
        "bias": np.asarray(L0_ffn_b).reshape(NE * DM),
        "g_attn": np.asarray(g_xattn).reshape(1),
        "g_ffn": np.asarray(g_ffn).reshape(1),
    }
    arrays = {name: np.ascontiguousarray(a) for name, a in arrays.items()}
    nc = bacc.Bacc("TRN2", target_bir_lowering=False, num_devices=1)
    args = {name: nc.dram_tensor(name, a.shape, mb.dt.from_np(a.dtype), kind="ExternalInput").ap()
            for name, a in arrays.items()}
    out = nc.dram_tensor("out", [NT, DM], F32, kind="ExternalOutput").ap()
    build(nc, out=out, **args)
    r = run(nc, [arrays], core_ids=[0])
    return r.results[0]["out"].reshape(NB, ROWS, DM)
```
